# Optimizing a Trainium2 kernel written in Bass

```python
import numpy as np
import jax
import jax.numpy as jnp

def _softmax(x, axis=-1):
    return jax.nn.softmax(x, axis=axis)

def _gelu(x):
    return jax.nn.gelu(x, approximate=True)

def _silu(x):
    return jax.nn.silu(x)

def _sigmoid(x):
    return jax.nn.sigmoid(x)

def _layernorm(x, axis=-1, eps=1e-05):
    m = jnp.mean(x, axis=axis, keepdims=True)
    v = jnp.var(x, axis=axis, keepdims=True)
    return (x - m) / jnp.sqrt(v + eps)

def _scatter_add(tgt, idx, src, axis=0):
    return tgt.at[idx].add(src)

def _segment_sum(src, seg, n):
    return jax.ops.segment_sum(src, seg, n)
kernel_name = 'mk_adaln_attn_ffn_d1_seqx_r8_6bf23b'

def setup_inputs(seed: int=0):
    np.random.seed(seed)
    _w = jnp.asarray

    def _rec_inputs():
        import jax
        import jax.numpy as jnp
        _rk = jax.random.key(seed)
        x = -0.000125 + 0.9999 * jax.random.normal(jax.random.fold_in(_rk, 1), (2, 512, 128), jnp.float32)
        _lenS = 512 - jax.random.randint(jax.random.fold_in(_rk, 7), (2,), 0, max(1, 512 // 4) + 1, jnp.int32)
        _lenS2 = 512 - jax.random.randint(jax.random.fold_in(_rk, 8), (2,), 0, max(1, 512 // 4) + 1, jnp.int32)
        cond_8 = jax.random.uniform(jax.random.fold_in(_rk, 11), (2, 8), jnp.float32, 0.0, 0.983423)
        return (x, cond_8)
    x, cond_8 = _rec_inputs()

    def _L0_cond_setup():
        import jax, jax.numpy as jnp
        import numpy as np
        B, S, D = (16, 256, 128)
        E, H = (8, 256)
        key = jax.random.key(seed)
        ks = jax.random.split(key, 8)
        scale = 0.02
        x = jax.random.normal(ks[0], (B, S, D), dtype=jnp.float32)
        opcode_onehot = jax.random.uniform(ks[1], (B, E), dtype=jnp.float32)
        W_up = jax.random.normal(ks[2], (E, H, D), dtype=jnp.float32) * scale
        b_up = jnp.zeros((E, H), dtype=jnp.float32)
        W_gate = jax.random.normal(ks[3], (E, H, D), dtype=jnp.float32) * scale
        b_gate = jnp.zeros((E, H), dtype=jnp.float32)
        W_down = jax.random.normal(ks[4], (E, D, H), dtype=jnp.float32) * scale
        b_down = jnp.zeros((E, D), dtype=jnp.float32)
        return {'x': x, 'opcode_onehot': opcode_onehot, 'W_up': W_up, 'b_up': b_up, 'W_gate': W_gate, 'b_gate': b_gate, 'W_down': W_down, 'b_down': b_down}
    _L0_cond_all = _L0_cond_setup()
    _L0_cond_in = {k: v for k, v in _L0_cond_all.items() if k in ('W_up', 'b_up', 'W_gate', 'b_gate', 'W_down', 'b_down')}
    del _L0_cond_all

    def _L0_attn_setup():
        import jax, jax.numpy as jnp
        import numpy as np
        from jax import lax
        B, S, E, H, KS = (2, 256, 128, 16, 3)
        DH = E // H
        key = jax.random.key(seed)
        ks = jax.random.split(key, 11)
        s = 1.0 / np.sqrt(E)
        sc = 1.0 / np.sqrt(H * KS)
        return {'query': jax.random.normal(ks[0], (B, S, E), jnp.float32), 'Wq': jax.random.uniform(ks[1], (E, E), jnp.float32, -s, s), 'bq': jax.random.uniform(ks[2], (E,), jnp.float32, -s, s), 'Wk': jax.random.uniform(ks[3], (E, E), jnp.float32, -s, s), 'bk': jax.random.uniform(ks[4], (E,), jnp.float32, -s, s), 'Wv': jax.random.uniform(ks[5], (E, E), jnp.float32, -s, s), 'bv': jax.random.uniform(ks[6], (E,), jnp.float32, -s, s), 'Wo': jax.random.uniform(ks[7], (E, E), jnp.float32, -s, s), 'bo': jax.random.uniform(ks[8], (E,), jnp.float32, -s, s), 'conv_w': jax.random.uniform(ks[9], (H, H, KS), jnp.float32, -sc, sc), 'conv_b': jax.random.uniform(ks[10], (H,), jnp.float32, -sc, sc)}
    _L0_attn_all = _L0_attn_setup()
    _L0_attn_in = {k: v for k, v in _L0_attn_all.items() if k in ('Wq', 'bq', 'Wk', 'bk', 'Wv', 'bv', 'Wo', 'bo', 'conv_w', 'conv_b')}
    del _L0_attn_all

    def _L0_cond2_setup():
        import jax, jax.numpy as jnp
        import numpy as np
        R = 16
        ALPHA = 32.0
        SCALING = ALPHA / R
        key = jax.random.key(seed)
        ks = jax.random.split(key, 6)
        B, T, C, O, E = (16, 1500, 128, 128, 8)
        x = jax.random.normal(ks[0], (B, T, C), dtype=jnp.float32)
        w = jax.random.uniform(ks[1], (B, E), dtype=jnp.float32)
        W_base = jax.random.normal(ks[2], (O, C), dtype=jnp.float32) * 0.02
        b_base = jax.random.normal(ks[3], (O,), dtype=jnp.float32) * 0.02
        As = jax.random.normal(ks[4], (E, R, C), dtype=jnp.float32) * 0.02
        Bs = jax.random.normal(ks[5], (E, O, R), dtype=jnp.float32) * 0.02
        return {'x': x, 'w': w, 'W_base': W_base, 'b_base': b_base, 'As': As, 'Bs': Bs}
    _L0_cond2_all = _L0_cond2_setup()
    _L0_cond2_in = {k: v for k, v in _L0_cond2_all.items() if k in ('W_base', 'b_base', 'As', 'Bs')}
    del _L0_cond2_all

    def _L0_ffn_setup():
        import jax, jax.numpy as jnp
        import numpy as np
        key = jax.random.key(seed)
        ks = jax.random.split(key, 5)
        B, Sq, M, E, H = (4, 256, 128, 8, 512)
        x = jax.random.normal(ks[0], (B, Sq, M), dtype=jnp.float32)
        wg = jax.random.normal(ks[1], (M, E), dtype=jnp.float32) * (1.0 / np.sqrt(M))
        w1 = jax.random.normal(ks[2], (E, M, H), dtype=jnp.float32) * (1.0 / np.sqrt(M))
        b1 = jnp.zeros((E, H), dtype=jnp.float32)
        w2 = jax.random.normal(ks[3], (E, H, M), dtype=jnp.float32) * (1.0 / np.sqrt(H))
        b2 = jnp.zeros((E, M), dtype=jnp.float32)
        return {'x': x, 'wg': wg, 'w1': w1, 'b1': b1, 'w2': w2, 'b2': b2}
    _L0_ffn_all = _L0_ffn_setup()
    _L0_ffn_in = {k: v for k, v in _L0_ffn_all.items() if k in ('wg', 'w1', 'b1', 'w2', 'b2')}
    del _L0_ffn_all
    return {'x': x, 'cond_8': cond_8, 'L0_cond_W_up': _L0_cond_in['W_up'], 'L0_cond_b_up': _L0_cond_in['b_up'], 'L0_cond_W_gate': _L0_cond_in['W_gate'], 'L0_cond_b_gate': _L0_cond_in['b_gate'], 'L0_cond_W_down': _L0_cond_in['W_down'], 'L0_cond_b_down': _L0_cond_in['b_down'], 'L0_attn_Wq': _L0_attn_in['Wq'], 'L0_attn_bq': _L0_attn_in['bq'], 'L0_attn_Wk': _L0_attn_in['Wk'], 'L0_attn_bk': _L0_attn_in['bk'], 'L0_attn_Wv': _L0_attn_in['Wv'], 'L0_attn_bv': _L0_attn_in['bv'], 'L0_attn_Wo': _L0_attn_in['Wo'], 'L0_attn_bo': _L0_attn_in['bo'], 'L0_attn_conv_w': _L0_attn_in['conv_w'], 'L0_attn_conv_b': _L0_attn_in['conv_b'], 'L0_cond2_W_base': _L0_cond2_in['W_base'], 'L0_cond2_b_base': _L0_cond2_in['b_base'], 'L0_cond2_As': _L0_cond2_in['As'], 'L0_cond2_Bs': _L0_cond2_in['Bs'], 'L0_ffn_wg': _L0_ffn_in['wg'], 'L0_ffn_w1': _L0_ffn_in['w1'], 'L0_ffn_b1': _L0_ffn_in['b1'], 'L0_ffn_w2': _L0_ffn_in['w2'], 'L0_ffn_b2': _L0_ffn_in['b2']}

def reference(x, cond_8, L0_cond_W_up, L0_cond_b_up, L0_cond_W_gate, L0_cond_b_gate, L0_cond_W_down, L0_cond_b_down, L0_attn_Wq, L0_attn_bq, L0_attn_Wk, L0_attn_bk, L0_attn_Wv, L0_attn_bv, L0_attn_Wo, L0_attn_bo, L0_attn_conv_w, L0_attn_conv_b, L0_cond2_W_base, L0_cond2_b_base, L0_cond2_As, L0_cond2_Bs, L0_ffn_wg, L0_ffn_w1, L0_ffn_b1, L0_ffn_w2, L0_ffn_b2):
    import jax
    import jax.numpy as jnp

    def _L0_cond_ref(x, opcode_onehot, W_up, b_up, W_gate, b_gate, W_down, b_down):
        import jax, jax.numpy as jnp
        import numpy as np
        B, S, D = (16, 256, 128)
        E, H = (8, 256)
        expert = jnp.argmax(opcode_onehot, axis=-1)
        wu, bu = (W_up[expert], b_up[expert])
        wg, bg = (W_gate[expert], b_gate[expert])
        wd, bd = (W_down[expert], b_down[expert])
        up = jnp.einsum('bsd,bhd->bsh', x, wu) + bu[:, None, :]
        gate = jnp.einsum('bsd,bhd->bsh', x, wg) + bg[:, None, :]
        hidden = jax.nn.silu(up) * gate
        out = jnp.einsum('bsh,bdh->bsd', hidden, wd) + bd[:, None, :]
        return out

    def _L0_attn_ref(query, Wq, bq, Wk, bk, Wv, bv, Wo, bo, conv_w, conv_b):
        import jax, jax.numpy as jnp
        import numpy as np
        from jax import lax
        B, S, E, H, KS = (2, 256, 128, 16, 3)
        DH = E // H
        b, s, e = query.shape
        h, dh = (H, DH)
        Q = (query @ Wq.T + bq).reshape(b, s, h, dh).transpose(0, 2, 1, 3)
        K = (query @ Wk.T + bk).reshape(b, s, h, dh).transpose(0, 2, 1, 3)
        V = (query @ Wv.T + bv).reshape(b, s, h, dh).transpose(0, 2, 1, 3)
        scores = jnp.einsum('bhqd,bhkd->bhqk', Q, K) / np.sqrt(dh).astype(np.float32)
        x = scores.transpose(0, 2, 1, 3).reshape(b * s, h, s)
        x = lax.conv_general_dilated(x, conv_w, window_strides=(1,), padding=[(KS // 2, KS // 2)], dimension_numbers=('NCW', 'OIW', 'NCW'))
        x = x + conv_b[None, :, None]
        scores = x.reshape(b, s, h, s).transpose(0, 2, 1, 3)
        weights = jax.nn.softmax(scores, axis=-1)
        out = jnp.einsum('bhqk,bhkd->bqhd', weights, V).reshape(b, s, e)
        return out @ Wo.T + bo

    def _L0_cond2_ref(x, w, W_base, b_base, As, Bs):
        import jax, jax.numpy as jnp
        import numpy as np
        R = 16
        ALPHA = 32.0
        SCALING = ALPHA / R
        out = jnp.einsum('btc,oc->bto', x, W_base) + b_base
        h = jnp.einsum('btc,erc->bter', x, As)
        lora = jnp.einsum('bter,eor,be->bto', h, Bs, w)
        return out + lora * SCALING

    def _L0_ffn_ref(x, wg, w1, b1, w2, b2):
        import jax, jax.numpy as jnp
        import numpy as np
        B, Sq, M = x.shape
        E = wg.shape[1]
        S = B * Sq
        C = S // E
        xt = x.reshape(S, M)
        gates = jax.nn.softmax(xt @ wg, axis=-1)
        expert_idx = jnp.argmax(gates, axis=-1)
        mask1 = jax.nn.one_hot(expert_idx, E, dtype=xt.dtype)
        locations = jnp.cumsum(mask1, axis=0) - 1.0
        pos = jnp.sum(locations * mask1, axis=1).astype(jnp.int32)
        keep = (pos < C).astype(xt.dtype)
        gate_val = jnp.sum(gates * mask1, axis=1) * keep
        slot = expert_idx.astype(jnp.int32) * C + jnp.clip(pos, 0, C - 1)
        disp = jnp.zeros((E * C, M), dtype=xt.dtype).at[slot].add(xt * keep[:, None])
        disp = disp.reshape(E, C, M)
        h = jax.nn.relu(jnp.einsum('ecm,emh->ech', disp, w1) + b1[:, None, :])
        eo = jnp.einsum('ech,ehm->ecm', h, w2) + b2[:, None, :]
        out = eo.reshape(E * C, M)[slot] * gate_val[:, None]
        return out.reshape(B, Sq, M)
    x = x + _L0_attn_ref(_L0_cond_ref(x, cond_8, L0_cond_W_up, L0_cond_b_up, L0_cond_W_gate, L0_cond_b_gate, L0_cond_W_down, L0_cond_b_down), L0_attn_Wq, L0_attn_bq, L0_attn_Wk, L0_attn_bk, L0_attn_Wv, L0_attn_bv, L0_attn_Wo, L0_attn_bo, L0_attn_conv_w, L0_attn_conv_b)
    x = x + _L0_ffn_ref(_L0_cond2_ref(x, cond_8, L0_cond2_W_base, L0_cond2_b_base, L0_cond2_As, L0_cond2_Bs), L0_ffn_wg, L0_ffn_w1, L0_ffn_b1, L0_ffn_w2, L0_ffn_b2)
    return x

_drawn_inputs = setup_inputs


def setup_inputs(seed=0):
    import zlib

    import numpy as np

    out = dict(_drawn_inputs(seed))
    spreads = {'L0_cond_b_up': (0.0, 0.8),
     'L0_cond_b_gate': (0.0, 0.8),
     'L0_cond_b_down': (0.0, 0.1),
     'L0_ffn_b1': (0.0, 0.701),
     'L0_ffn_b2': (0.0, 0.481)}
    factors = {'L0_cond_W_up': 8.0,
     'L0_cond_W_gate': 8.0,
     'L0_cond_W_down': 8.0,
     'L0_attn_Wq': 8.0,
     'L0_attn_bq': 8.0,
     'L0_attn_Wk': 8.0,
     'L0_attn_bk': 200.0,
     'L0_attn_conv_w': 8.0,
     'L0_attn_conv_b': 64.0,
     'L0_cond2_b_base': 4.177,
     'L0_cond2_As': 2.959,
     'L0_cond2_Bs': 2.883,
     'L0_attn_bv': 2.744}
    for name, (base, spread) in spreads.items():
        noise = np.random.default_rng([zlib.crc32(name.encode()), seed]).standard_normal(out[name].shape)
        drawn = base * np.exp(spread * noise) if base else spread * noise
        out[name] = jnp.asarray(drawn.astype(out[name].dtype))
    for name, factor in factors.items():
        out[name] = (out[name] * factor).astype(out[name].dtype)
    return out
```

```python
import numpy as np
import concourse.bass as bass
from concourse import mybir
from contextlib import ExitStack

B, S, C = 2, 512, 128
H, DH, TAPS = 16, 8, 3
E, HE, HID = 8, 256, 512
T = B * S
NT = T // 128
QT = S // 128
G = 4
NG = H // G
U = G * QT
RING = 8
AHEAD = 4
CAP = T // E
VW = 32
NJ = HID // 128

BQ, BK, BO, BB, CW = 0, 1, 2, 3, 4
CB = CW + H * TAPS
B1 = CB + H
WG = B1 + E * NJ
LW = WG + E
BV = LW + B
NCOLS = BV + C
WU, WGT, WD, EB = 0, HE, 2 * HE, 2 * HE + 2 * C
EW = EB + 5
ID, TRI, IO8, IP, IOTA = 0, 128, 256, 264, 272
NCONST = IOTA + E * CAP


def build(nc, cond, wexp, xT, wqkvo, lora, cols, b2row, w1, w2, consts, out):
    f32, f32r = mybir.dt.float32, mybir.dt.float32r
    u32 = mybir.dt.uint32
    ALU, ACT, AX = mybir.AluOpType, mybir.ActivationFunctionType, mybir.AxisListType

    with ExitStack() as ctx:
        def sb(name, shape, dt=f32):
            return ctx.enter_context(nc.sbuf_tensor(name, shape, dt))

        def sem(name):
            return ctx.enter_context(nc.semaphore(name))

        banks = [ctx.enter_context(nc.psum_tensor(n, [128, 512], f32))
                 for n in ("sc0", "sc1", "sc2", "sc3", "tp0", "tp1", "pvbank", "misc")]
        SC, TP, PV, MISC = banks[0:4], banks[4:6], banks[6], banks[7]

        condS = sb("condS", [1, B * E])
        cmax = sb("cmax", [1, B * 8])
        cidx = sb("cidx", [1, B * 8], u32)
        we = sb("we", [128, B, EW])
        hb = sb("hb", [128, B, 2])
        xTs = sb("xTs", [128, T])
        wq = sb("wq", [128, 4, 128])
        lo_w = sb("lo_w", [128, 3, 128])
        bs = sb("bs", [128, B, 128])
        weff = sb("weff", [128, B, 128])
        col = sb("col", [128, NCOLS])
        b2s = sb("b2s", [1, E * C])
        w1s = sb("w1s", [128, E, HID])
        w2s = sb("w2s", [128, E, NJ, C])
        cst = sb("cst", [128, NCONST])
        ones = sb("ones", [128, 128])
        ident, tri = cst[:, ID:ID + 128], cst[:, TRI:TRI + 128]

        RAW = sb("RAW", [128, NG, S])
        yT, q32 = RAW[:, 0:B, :], RAW[:, B, :]
        Qh = sb("Qh", [128, B, S], f32r)
        Ql = sb("Ql", [128, B, S], f32r)
        Kp = sb("Kp", [128, B, S + 2])
        V = sb("V", [128, B, QT, H, DH])
        Vst = sb("Vst", [128, QT, G, VW])
        cwS = sb("cwS", [128, 2, TAPS])
        ta = sb("ta", [128, S])
        tc_ = sb("tc_", [128, S])
        td = sb("td", [128, 2, S])
        kc = sb("kc", [128, S])
        Kh = sb("Kh", [128, 2, S], f32r)
        Kl = sb("Kl", [128, 2, S], f32r)
        spare = sb("spare", [128, 4])
        nbias = sb("nbias", [128, RING])
        Pb = sb("Pb", [128, RING, S])
        PT = sb("PT", [128, G, QT, S])
        rec = sb("rec", [128, QT, H])
        O = sb("O", [128, QT, C])
        OT = sb("OT", [128, S])
        x1T = sb("x1T", [128, S])
        X1 = sb("X1", [128, NT, C])
        zT = sb("zT", [128, S])
        Zh = sb("Zh", [128, NT, C], f32r)
        Zl = sb("Zl", [128, NT, C], f32r)
        lg = sb("lg", [128, QT, E])
        es = sb("es", [128, QT, E])
        eq = sb("eq", [128, QT, E])
        mask = sb("mask", [128, NT, E])
        r1 = sb("r1", [128, 8, QT])
        slot = sb("slot", [128, NT])
        gval = sb("gval", [128, NT])
        diag = OT[:, :].rearrange("p (q t) -> p q t", q=QT)
        SR = sb("SR", [128, T])
        D = sb("D", [128, NT, T], f32r)
        EOh, EOl = Zh, Zl

        flat = PT[:, :, :, :].rearrange("p g k s -> p (g k s)")
        Ub = [[flat[:, (4 * b + i) * 512:(4 * b + i + 1) * 512] for i in range(2)] for b in range(B)]
        Tb = [[flat[:, (4 * b + 2 + i) * 512:(4 * b + 3 + i) * 512] for i in range(2)] for b in range(B)]
        Sb_ = [[flat[:, 4096 + (4 * b + i) * 512:4096 + (4 * b + i + 1) * 512] for i in range(2)] for b in range(B)]
        Hb = [[flat[:, 4096 + (4 * b + 2 + i) * 512:4096 + (4 * b + 3 + i) * 512] for i in range(2)] for b in range(B)]
        DT = flat[:, 0:1024]
        HT = [flat[:, 1024 + 512 * i:1536 + 512 * i].rearrange("p (j s) -> p j s", j=NJ) for i in range(2)]
        CT = flat[:, 2048:3072]
        OUT = flat[:, 3072:4096].rearrange("p (t m) -> p t m", t=NT)

        names = """spare cond cmax cidx we0 we1 xt wq lora cols b2 w1 w2 cst outd
            hb bsc ones kpad vpad wefmm wefe
            mlp ut sm hm ymm yev qmm kmm vmm qev qhi qlo kev vev
            cw ac d kc hi lo sc mx ex tp evd eva vst pv raw
            otr rcp on o2t ote wo x1 xtr xte zmm zte ztr zhi zlo lgm nl nla esr nr msk cum rt
            slt dg srm sre disp0 dsp dtea dted hmm heva hevd eom eoh eol dt2 cmb ctea cted ftr fo""".split()
        s = {n: sem("s_" + n) for n in names}

        block = ctx.enter_context(nc.Block())

        @block.sync
        def _(sp):
            sp.dma_start(condS[:, :], cond).then_inc(s["cond"], 16)
            sp.dma_start(xTs[:, :], xT).then_inc(s["xt"], 16)
            sp.wait_ge(s["cidx"], B)
            for b in range(B):
                e = sp.value_load(cidx[0:1, 8 * b:8 * b + 1], min_val=0, max_val=E - 1)
                sp.dma_start(we[:, b:b + 1, :], wexp[bass.ds(e, 1), :, :].rearrange("e p n -> p e n"))\
                    .then_inc(s[f"we{b}"], 16)
            sp.dma_start(w1s[:, :, :], w1).then_inc(s["w1"], 16)
            sp.dma_start(w2s[:, :, :, :], w2).then_inc(s["w2"], 16)
            sp.dma_start(b2s[:, :], b2row).then_inc(s["b2"], 16)
            for t in range(NT):
                sp.wait_ge(s["fo"], t + 1)
                sp.dma_start(out[t * 128:(t + 1) * 128, :], OUT[:, t, :]).then_inc(s["outd"], 16)
            sp.wait_ge(s["outd"], 16 * NT)

        @block.gpsimd
        def _(pool):
            pool.memset(ones[:, :], 1.0).then_inc(s["ones"], 1)
            for b in range(B):
                pool.memset(Kp[:, b, 0:1], 0.0).then_inc(s["kpad"], 1)
                pool.memset(Kp[:, b, S + 1:S + 2], 0.0).then_inc(s["kpad"], 1)
            pool.memset(Vst[:, :, :, DH:DH + 1], 1.0).then_inc(s["vpad"], 1)
            pool.memset(Vst[:, :, :, DH + 1:VW], 0.0).then_inc(s["vpad"], 1)
            pool.wait_ge(s["cols"], 16)

            def fetch_taps(hd, o, n):
                src = col[:, CW + TAPS * o:CW + TAPS * (o + 1)] if isinstance(o, int) else \
                    col[:, bass.ds(CW + TAPS * o, TAPS)]
                pool.wait_ge(s["d"], hd)
                pool.tensor_copy(cwS[:, n, :], src).then_inc(s["cw"], 1)

            def low_half(hd, n):
                pool.wait_ge(s["cw"], hd + 3)
                pool.wait_ge(s["hi"], hd + 1)
                pool.tensor_tensor(Kl[:, n, :], kc[:, :], Kh[:, n, :].bitcast(f32), ALU.subtract)\
                    .then_inc(s["lo"], 1)

            def outer_taps(hd, b, n):
                pool.tensor_scalar(ta[:, :], Kp[:, b, 0:S], cwS[:, n, 0:1], 1.0, ALU.mult, ALU.mult)\
                    .then_inc(s["ac"], 1)
                pool.tensor_scalar(tc_[:, :], Kp[:, b, 2:S + 2], cwS[:, n, 2:3], 1.0, ALU.mult, ALU.mult)\
                    .then_inc(s["ac"], 1)
                pool.wait_ge(s["ac"], 2 * hd + 2)
                if not isinstance(hd, int) or hd >= 2:
                    pool.wait_ge(s["kc"], hd - 1)
                pool.tensor_tensor(td[:, n, :], ta[:, :], tc_[:, :], ALU.add).then_inc(s["d"], 1)

            pool.wait_ge(s["kpad"], 2 * B)
            pool.wait_ge(s["kev"], 1)
            for hd in range(2):
                fetch_taps(hd, hd, hd)
                pool.wait_ge(s["cw"], hd + 1)
                outer_taps(hd, 0, hd)
            for hd in range(2):
                fetch_taps(hd + 2, hd + 2, hd)
                low_half(hd, hd)
                outer_taps(hd + 2, 0, hd)
            pool.wait_ge(s["kev"], 2)

            def group(b, g):
                for j in range(G):
                    hd = H * b + G * g + j
                    o = G * g + j + 4
                    over = isinstance(g, int) and o >= H
                    if isinstance(g, int) and hd + 4 >= B * H:
                        if hd + 2 < B * H:
                            pool.wait_ge(s["hi"], hd + 3)
                            pool.tensor_tensor(Kl[:, j % 2, :], kc[:, :], Kh[:, j % 2, :].bitcast(f32),
                                               ALU.subtract).then_inc(s["lo"], 1)
                        continue
                    fetch_taps(hd + 4, o - H if over else o, j % 2)
                    low_half(hd + 2, j % 2)
                    outer_taps(hd + 4, b + 1 if over else b, j % 2)

            for b in range(B):
                with pool.Fori(0, NG - 1) as g:
                    group(b, g)
                group(b, NG - 1)

        @block.scalar
        def _(act):
            act.dma_start(col[:, :], cols).then_inc(s["cols"], 16)
            act.dma_start(wq[:, :, :], wqkvo).then_inc(s["wq"], 16)
            act.dma_start(lo_w[:, :, :], lora).then_inc(s["lora"], 16)
            act.dma_start(cst[:, :], consts).then_inc(s["cst"], 16)

            def high_first(hd):
                act.wait_ge(s["kc"], hd + 1)
                act.activation(Kh[:, hd, :], kc[:, :], ACT.Copy).then_inc(s["hi"], 1)

            act.wait_ge(s["spare"], 1)
            act.activation(spare[:, 2:3], spare[:, 0:1], ACT.Copy).then_inc(s["ex"], 1)
            act.activation(spare[:, 3:4], spare[:, 1:2], ACT.Copy).then_inc(s["eva"], 1)

            for b in range(B):
                act.wait_ge(s["hb"], b + 1)
                for i in range(2):
                    act.wait_ge(s["mlp"], 4 * b + i + 1)
                    act.activation(Ub[b][i], SC[i][:, :], ACT.Identity, bias=hb[:, b, i:i + 1], scale=0.5)\
                        .then_inc(s["ut"], 1)
                    act.activation(Tb[b][i], SC[i][:, :], ACT.Tanh, bias=hb[:, b, i:i + 1], scale=0.5)\
                        .then_inc(s["ut"], 1)
                if b == 1:
                    high_first(0)
                act.wait_ge(s["kmm"], b + 1)
                act.activation(Kp[:, b, 1:S + 1], PV[:, :], ACT.Identity, bias=col[:, BK:BK + 1])\
                    .then_inc(s["kev"], 1)
                act.wait_ge(s["qev"], b + 1)
                act.activation(Qh[:, b, :], q32[:, :], ACT.Copy).then_inc(s["qhi"], 1)
            high_first(1)

            def high_half(hd, n):
                act.wait_ge(s["kc"], hd + 1)
                act.wait_ge(s["sc"], QT * (hd - 1))
                act.activation(Kh[:, n, :], kc[:, :], ACT.Copy).then_inc(s["hi"], 1)

            def exp(n, k):
                act.wait_ge(s["mx"], n + 2)
                act.activation(Pb[:, k, :], Pb[:, k, :], ACT.Exp, bias=nbias[:, k:k + 1], scale=-1.0)\
                    .then_inc(s["ex"], 1)

            def stage_values(b, g):
                gi = NG * b + g
                act.wait_ge(s["pv"], gi + 1)
                src = V[:, b, :, bass.ds(G * g, G), :] if not isinstance(g, int) else \
                    V[:, b, :, G * g:G * g + G, :]
                act.activation(Vst[:, :, :, 0:DH], src, ACT.Copy).then_inc(s["vst"], 1)

            def group(b, g):
                n0 = U * (NG * b + g)
                for u in range(U):
                    hd = H * b + G * g + u // QT
                    if u % QT == 0 and (not isinstance(g, int) or hd + 2 < B * H):
                        high_half(hd + 2, (u // QT) % 2)
                    if not isinstance(g, int) or n0 + u + AHEAD < U * NG * B:
                        exp(n0 + u + AHEAD, (u + AHEAD) % RING)
                    if u % 2 == 1:
                        act.wait_ge(s["tp"], n0 + u + 2)
                        act.wait_ge(s["pv"], NG * b + g + 1)
                        act.activation(PT[:, u // QT, :, (u % QT) * 128:(u % QT + 1) * 128],
                                       TP[1][:, :].rearrange("p (k q) -> p k q", k=QT), ACT.Copy)\
                            .then_inc(s["eva"], 1)
                    if u == 2:
                        stage_values(b, g)

            act.wait_ge(s["vev"], B)
            act.wait_ge(s["vpad"], 2)
            for k in range(AHEAD):
                exp(k, k)

            def after(b):
                act.wait_ge(s["o2t"], b + 1)
                act.activation(OT[:, :], MISC[:, :], ACT.Copy).then_inc(s["ote"], 1)
                act.wait_ge(s["xtr"], b + 1)
                act.activation(X1[:, QT * b:QT * (b + 1), :], MISC[:, :].rearrange("p (t m) -> p t m", t=QT),
                               ACT.Copy).then_inc(s["xte"], 1)
                act.wait_ge(s["ztr"], b + 1)
                act.activation(Zh[:, QT * b:QT * (b + 1), :], MISC[:, :].rearrange("p (t m) -> p t m", t=QT),
                               ACT.Copy).then_inc(s["zhi"], 1)
                act.wait_ge(s["nl"], b + 1)
                act.activation(es[:, :, :], lg[:, :, :], ACT.Exp).then_inc(s["nla"], 1)
                act.wait_ge(s["srm"], b + 1)
                act.activation(SR[:, S * b:S * (b + 1)], MISC[:, :], ACT.Copy).then_inc(s["sre"], 1)

            for b in range(B):
                with act.Fori(0, NG - 1) as g:
                    group(b, g)
                group(b, NG - 1)
                after(b)

            act.wait_ge(s["dsp"], 1)
            act.activation(DT[:, 0:512], SC[0][:, :], ACT.Copy).then_inc(s["dtea"], 1)
            for e in range(E):
                if e % 2 == 0:
                    act.wait_ge(s["hmm"], e + 1)
                    if e >= 2:
                        act.wait_ge(s["eom"], e - 1)
                    for j in range(NJ):
                        act.activation(HT[0][:, j, :], SC[2][:, j * 128:(j + 1) * 128], ACT.Relu,
                                       bias=col[:, B1 + NJ * e + j:B1 + NJ * e + j + 1]).then_inc(s["heva"], 1)
                act.wait_ge(s["eom"], e + 1)
                act.activation(EOh[:, e, :], TP[e % 2][:, 0:C], ACT.Copy).then_inc(s["eoh"], 1)
            act.wait_ge(s["cmb"], 1)
            act.activation(CT[:, 0:512], PV[:, :], ACT.Copy).then_inc(s["ctea"], 1)

        @block.vector
        def _(dve):
            dve.memset(nbias[:, 0:1], 0.0).then_inc(s["evd"], 1)
            dve.memset(nbias[:, 1:2], 0.0).then_inc(s["raw"], 1)
            dve.memset(nbias[:, 2:3], 0.0).then_inc(s["mx"], 1)
            dve.memset(spare[:, 0:2], 0.0).then_inc(s["spare"], 1)
            dve.wait_ge(s["cond"], 16)
            for b in range(B):
                dve.max(cmax[:, 8 * b:8 * b + 8], condS[:, E * b:E * b + E]).then_inc(s["cmax"], 1)
            for b in range(B):
                dve.wait_ge(s["cmax"], b + 1)
                dve.max_index(cidx[:, 8 * b:8 * b + 8], cmax[:, 8 * b:8 * b + 8],
                              condS[:, E * b:E * b + E]).then_inc(s["cidx"], 1)
            dve.wait_ge(s["lora"], 16)
            dve.wait_ge(s["cols"], 16)
            for b in range(B):
                dve.tensor_scalar(bs[:, b, :], lo_w[:, 1, :], col[:, LW + b:LW + b + 1], 2.0,
                                  ALU.mult, ALU.mult).then_inc(s["bsc"], 1)
            for b in range(B):
                dve.wait_ge(s[f"we{b}"], 16)
                dve.tensor_scalar(hb[:, b, :], we[:, b, EB:EB + 2], 0.5, None, ALU.mult).then_inc(s["hb"], 1)
            for b in range(B):
                dve.wait_ge(s["wefmm"], b + 1)
                dve.tensor_tensor(weff[:, b, :], MISC[:, 0:C], lo_w[:, 2, :], ALU.add).then_inc(s["wefe"], 1)
            def middle_tap(hd, b, o, n):
                at = CW + TAPS * o + 1
                w = col[:, at:at + 1] if isinstance(o, int) else col[:, bass.ds(at, 1)]
                dve.wait_ge(s["d"], hd + 1)
                dve.wait_ge(s["lo"], hd)
                dve.scalar_tensor_tensor(kc[:, :], Kp[:, b, 1:S + 1], w, td[:, n, :], ALU.mult, ALU.add)\
                    .then_inc(s["kc"], 1)

            for b in range(B):
                for i in range(2):
                    dve.wait_ge(s["ut"], 4 * b + 2 * i + 2)
                    dve.scalar_tensor_tensor(Sb_[b][i], Tb[b][i], 1.0, Ub[b][i], ALU.add, ALU.mult)\
                        .then_inc(s["sm"], 1)
                if b == 1:
                    middle_tap(0, 0, 0, 0)
                for i in range(2):
                    dve.wait_ge(s["sm"], 2 * b + i + 1)
                    dve.wait_ge(s["mlp"], 4 * b + 3 + i)
                    dve.scalar_tensor_tensor(Hb[b][i], SC[2 + i][:, :], we[:, b, EB + 2 + i:EB + 3 + i],
                                             Sb_[b][i], ALU.add, ALU.mult).then_inc(s["hm"], 1)
                dve.wait_ge(s["ymm"], b + 1)
                dve.tensor_scalar(yT[:, b, :], TP[0][:, :], we[:, b, EB + 4:EB + 5], None, ALU.add)\
                    .then_inc(s["yev"], 1)
                dve.wait_ge(s["qmm"], b + 1)
                if b:
                    dve.wait_ge(s["qhi"], b)
                    dve.wait_ge(s["qlo"], b)
                dve.tensor_scalar(q32[:, :], TP[1][:, :], col[:, BQ:BQ + 1], -float(DH) ** -0.5,
                                  ALU.add, ALU.mult).then_inc(s["qev"], 1)
                dve.wait_ge(s["vmm"], b + 1)
                bv = col[:, BV:BV + C].rearrange("p (h d) -> p h d", d=DH)
                for k in range(QT):
                    v = dve.tensor_tensor(V[:, b, k, :, :], MISC[:, k * 128:(k + 1) * 128]
                                          .rearrange("p (h d) -> p h d", d=DH), bv, ALU.add)
                v.then_inc(s["vev"], 1)
                dve.wait_ge(s["qhi"], b + 1)
                dve.tensor_tensor(Ql[:, b, :], q32[:, :], Qh[:, b, :].bitcast(f32), ALU.subtract)\
                    .then_inc(s["qlo"], 1)

            def maximum(n, k, o):
                cb = col[:, CB + o:CB + o + 1] if isinstance(o, int) else col[:, bass.ds(CB + o, 1)]
                dve.wait_ge(s["sc"], n + 1)
                dve.tensor_scalar(Pb[:, k, :], SC[k % 4][:, :], cb, None, ALU.subtract, ALU.min,
                                  accum_out=nbias[:, k:k + 1]).then_inc(s["mx"], 1)

            def group(b, g):
                n0 = U * (NG * b + g)
                for u in range(U):
                    m = u + AHEAD
                    go = not isinstance(g, int) or n0 + m < U * NG * B
                    over = isinstance(g, int) and G * g + m // QT >= H
                    if go:
                        maximum(n0 + m, m % RING, G * g + m // QT - (H if over else 0))
                    if u % 2 == 0:
                        dve.wait_ge(s["tp"], n0 + u + 2)
                        dve.wait_ge(s["pv"], NG * b + g + 1)
                        dve.tensor_copy(PT[:, u // QT, :, (u % QT) * 128:(u % QT + 1) * 128],
                                        TP[0][:, :].rearrange("p (k q) -> p k q", k=QT))\
                            .then_inc(s["evd"], 1)
                    hd = H * b + G * g + u // QT
                    if u % QT == 2 and (not isinstance(g, int) or hd + 3 < B * H):
                        nxt = isinstance(g, int) and G * g + u // QT + 3 >= H
                        middle_tap(hd + 3, b + 1 if nxt else b, G * g + u // QT + 3 - (H if nxt else 0),
                                   (u // QT + 1) % 2)
                dve.wait_ge(s["pv"], NG * b + g + 2)
                dst = RAW[:, bass.ds(g, 1), :] if not isinstance(g, int) else RAW[:, g:g + 1, :]
                dve.tensor_copy(dst, PV[:, :].rearrange("p (a q) -> p a q", a=1)).then_inc(s["raw"], 1)

            middle_tap(1, 0, 1, 1)
            for k in range(AHEAD):
                maximum(k, k, 0)
            middle_tap(2, 0, 2, 0)

            def after(b):
                tiles = slice(QT * b, QT * (b + 1))
                for q in range(QT):
                    dve.wait_ge(s["otr"], QT * b + q + 1)
                    t = MISC[:, :].rearrange("p (h w) -> p h w", w=VW)
                    if b:
                        dve.wait_ge(s["o2t"], b)
                    dve.reciprocal(rec[:, q, :], t[:, :, DH]).then_inc(s["rcp"], 1)
                    dve.wait_ge(s["rcp"], QT * b + q + 1)
                    r = rec[:, q, :].rearrange("p (h a) -> p h a", a=1)
                    dve.tensor_tensor(O[:, q, :].rearrange("p (h d) -> p h d", d=DH), t[:, :, 0:DH],
                                      r.broadcast_to([128, H, DH]), ALU.mult).then_inc(s["on"], 1)
                dve.wait_ge(s["wo"], b + 1)
                dve.scalar_tensor_tensor(x1T[:, :], MISC[:, :], col[:, BO:BO + 1], xTs[:, S * b:S * (b + 1)],
                                         ALU.add, ALU.add).then_inc(s["x1"], 1)
                dve.wait_ge(s["zmm"], b + 1)
                dve.tensor_scalar(zT[:, :], MISC[:, :], col[:, BB:BB + 1], None, ALU.add).then_inc(s["zte"], 1)
                dve.wait_ge(s["zhi"], b + 1)
                dve.tensor_tensor(Zl[:, tiles, :], MISC[:, :].rearrange("p (t m) -> p t m", t=QT),
                                  Zh[:, tiles, :].bitcast(f32), ALU.subtract).then_inc(s["zlo"], 1)
                n = [0]

                def step(ins):
                    n[0] += 1
                    ins.then_inc(s["nr"], 1)
                    dve.wait_ge(s["nr"], 14 * b + n[0])

                def over_experts(a):
                    return a.rearrange("p (t a) -> p t a", a=1).broadcast_to([128, QT, E])

                io8 = cst[:, IO8:IO8 + E].rearrange("p (a e) -> p a e", a=1).broadcast_to([128, QT, E])
                lmax, ssum, rs, gmax, idx, pos, keep, s1 = (r1[:, i, :] for i in range(8))
                L = MISC[:, 0:QT * E].rearrange("p (t e) -> p t e", e=E)
                dve.wait_ge(s["lgm"], b + 1)
                step(dve.tensor_reduce(lmax, L, AX.X, ALU.max))
                dve.tensor_tensor(lg[:, :, :], L, over_experts(lmax), ALU.subtract).then_inc(s["nl"], 1)
                dve.wait_ge(s["nla"], b + 1)
                step(dve.tensor_reduce(ssum, es[:, :, :], AX.X, ALU.add))
                step(dve.reciprocal(rs, ssum))
                step(dve.tensor_tensor(es[:, :, :], es[:, :, :], over_experts(rs), ALU.mult))
                step(dve.tensor_reduce(gmax, es[:, :, :], AX.X, ALU.max))
                step(dve.tensor_tensor(eq[:, :, :], es[:, :, :], over_experts(gmax), ALU.is_equal))
                step(dve.scalar_tensor_tensor(eq[:, :, :], eq[:, :, :], -float(E), io8, ALU.mult, ALU.add))
                step(dve.tensor_reduce(idx, eq[:, :, :], AX.X, ALU.min))
                step(dve.tensor_scalar(s1, idx, float(E), None, ALU.add))
                dve.tensor_tensor(mask[:, tiles, :], io8, over_experts(s1), ALU.is_equal).then_inc(s["msk"], 1)
                dve.wait_ge(s["cum"], b + 1)
                cum = MISC[:, 64:64 + QT * E].rearrange("p (t e) -> p t e", e=E)
                step(dve.tensor_tensor(eq[:, :, :], cum, mask[:, tiles, :], ALU.mult))
                step(dve.tensor_reduce(pos, eq[:, :, :], AX.X, ALU.add))
                step(dve.tensor_scalar(keep, pos, float(CAP), None, ALU.is_le))
                dve.tensor_tensor(gval[:, tiles], gmax, keep, ALU.mult).then_inc(s["rt"], 1)
                step(dve.scalar_tensor_tensor(s1, idx, float(CAP), pos, ALU.mult, ALU.add))
                step(dve.tensor_tensor(s1, s1, keep, ALU.mult))
                dve.tensor_scalar(slot[:, tiles], s1, -1.0, None, ALU.add).then_inc(s["slt"], 1)
                dve.wait_ge(s["slt"], b + 1)
                if b:
                    dve.wait_ge(s["srm"], b)
                for q in range(QT):
                    dve.tensor_scalar(diag[:, q, :], ident, slot[:, QT * b + q:QT * b + q + 1], None, ALU.mult)\
                        .then_inc(s["dg"], 1)
                for q in range(QT):
                    t = QT * b + q
                    dve.tensor_scalar(D[:, t, :], cst[:, IOTA:IOTA + T], slot[:, t:t + 1], None, ALU.is_equal)\
                        .then_inc(s["disp0"], 1)

            for b in range(B):
                with dve.Fori(0, NG - 1) as g:
                    group(b, g)
                group(b, NG - 1)
                if b == 0:
                    dve.wait_ge(s["cst"], 16)
                after(b)

            dve.wait_ge(s["dsp"], 2)
            dve.tensor_copy(DT[:, 512:1024], SC[1][:, :]).then_inc(s["dted"], 1)
            dve.wait_ge(s["sre"], B)

            def spread(e):
                dve.tensor_scalar(D[:, e, :], SR[:, :], cst[:, IP + e:IP + e + 1], None, ALU.is_equal)\
                    .then_inc(s["dt2"], 1)

            for e in range(E):
                if e % 2 == 1:
                    dve.wait_ge(s["hmm"], e + 1)
                    if e >= 3:
                        dve.wait_ge(s["eom"], e - 1)
                    for j in range(NJ):
                        dve.tensor_scalar(HT[1][:, j, :], SC[3][:, j * 128:(j + 1) * 128],
                                          col[:, B1 + NJ * e + j:B1 + NJ * e + j + 1], 0.0, ALU.add, ALU.max)\
                            .then_inc(s["hevd"], 1)
                spread(e)
                dve.wait_ge(s["eoh"], e + 1)
                dve.tensor_tensor(EOl[:, e, :], TP[e % 2][:, 0:C], EOh[:, e, :].bitcast(f32), ALU.subtract)\
                    .then_inc(s["eol"], 1)
            dve.wait_ge(s["cmb"], 2)
            dve.tensor_copy(CT[:, 512:1024], MISC[:, :]).then_inc(s["cted"], 1)
            for t in range(NT):
                dve.wait_ge(s["ftr"], t // QT + 1)
                bank = SC[t // QT]
                dve.scalar_tensor_tensor(OUT[:, t, :], bank[:, (t % QT) * 128:(t % QT + 1) * 128],
                                         gval[:, t:t + 1], X1[:, t, :], ALU.mult, ALU.add).then_inc(s["fo"], 1)

        @block.tensor
        def _(pe):
            pe.wait_ge(s["lora"], 16)
            for b in range(B):
                pe.wait_ge(s["bsc"], b + 1)
                if b:
                    pe.wait_ge(s["wefe"], b)
                pe.matmul(MISC[:, 0:C], lo_w[:, 0, :], bs[:, b, :], start=True, stop=True).then_inc(s["wefmm"], 1)
            pe.wait_ge(s["xt"], 16)
            pe.wait_ge(s["wq"], 16)
            for b in range(B):
                x = xTs[:, S * b:S * (b + 1)]
                pe.wait_ge(s[f"we{b}"], 16)
                for i in range(4):
                    if b:
                        if i < 2:
                            pe.wait_ge(s["ut"], 4 * (b - 1) + 2 * i + 2)
                        else:
                            pe.wait_ge(s["hm"], 2 * (b - 1) + i - 1)
                    pe.matmul(SC[i][:, :], we[:, b, i * 128:(i + 1) * 128], x, start=True, stop=True)\
                        .then_inc(s["mlp"], 1)
                if b:
                    pe.wait_ge(s["yev"], b)
                for i in range(2):
                    pe.wait_ge(s["hm"], 2 * b + i + 1)
                    mm = pe.matmul(TP[0][:, :], we[:, b, WD + i * C:WD + (i + 1) * C], Hb[b][i],
                                   start=(i == 0), stop=(i == 1))
                mm.then_inc(s["ymm"], 1)
                pe.wait_ge(s["yev"], b + 1)
                if b:
                    pe.wait_ge(s["kev"], b)
                pe.matmul(PV[:, :], wq[:, 1, :], yT[:, b, :], start=True, stop=True).then_inc(s["kmm"], 1)
                if b:
                    pe.wait_ge(s["qev"], b)
                pe.matmul(TP[1][:, :], wq[:, 0, :], yT[:, b, :], start=True, stop=True).then_inc(s["qmm"], 1)
                if b == 0:
                    pe.wait_ge(s["wefe"], B)
                else:
                    pe.wait_ge(s["vev"], b)
                for k in range(QT):
                    mm = pe.matmul(MISC[:, k * 128:(k + 1) * 128], yT[:, b, k * 128:(k + 1) * 128], wq[:, 2, :],
                                   start=True, stop=True)
                mm.then_inc(s["vmm"], 1)

            def scores(n, hd, b, u):
                k, q = u % 4, u % QT
                qh, ql = Qh[:, b, q * 128:(q + 1) * 128], Ql[:, b, q * 128:(q + 1) * 128]
                h2 = (u // QT) % 2
                if q == 0:
                    pe.wait_ge(s["hi"], hd + 1)
                    pe.wait_ge(s["lo"], hd + 1)
                pe.wait_ge(s["mx"], n - 2)
                pe.matmul(SC[k][:, :], ql, Kh[:, h2, :], start=True, stop=False)
                pe.matmul(SC[k][:, :], qh, Kl[:, h2, :], start=False, stop=False)
                pe.matmul(SC[k][:, :], qh, Kh[:, h2, :], start=False, stop=True).then_inc(s["sc"], 1)

            def group(b, g):
                gi = NG * b + g
                n0 = U * gi
                for u in range(U):
                    m = u + AHEAD
                    if not isinstance(g, int) or n0 + m < U * NG * B:
                        over = isinstance(g, int) and g == NG - 1 and m >= U
                        scores(n0 + m, H * b + G * g + m // QT, b + 1 if over else b, m)
                    pe.wait_ge(s["ex"], n0 + u + 2)
                    if u % 2 == 0:
                        pe.wait_ge(s["evd"], (U // 2) * gi + u // 2 + 1)
                    else:
                        pe.wait_ge(s["eva"], (U // 2) * gi + u // 2 + 1)
                    for k in range(QT):
                        mm = pe.transpose(TP[u % 2][:, k * 128:(k + 1) * 128],
                                          Pb[:, u % RING, k * 128:(k + 1) * 128], ident)
                    mm.then_inc(s["tp"], 1)
                pe.wait_ge(s["evd"], (U // 2) * gi + U // 2 + 1)
                pe.wait_ge(s["eva"], (U // 2) * gi + U // 2 + 1)
                pe.wait_ge(s["vst"], gi + 1)
                pe.wait_ge(s["raw"], gi + 1)
                for k in range(QT):
                    for j in range(G):
                        mm = pe.matmul(PV[32 * j:32 * j + VW, :], Vst[:, k, j, :], PT[:, j, k, :],
                                       start=(k == 0), stop=(k == QT - 1))
                mm.then_inc(s["pv"], 1)

            def after(b):
                pe.wait_ge(s["raw"], NG * (b + 1) + 1)
                for q in range(QT):
                    if q or b:
                        pe.wait_ge(s["on"] if q else s["sre"], QT * b + q if q else b)
                    for g in range(NG):
                        mm = pe.transpose(MISC[:, g * 128:(g + 1) * 128], RAW[:, g, q * 128:(q + 1) * 128], ident)
                    mm.then_inc(s["otr"], 1)
                pe.wait_ge(s["on"], QT * (b + 1))
                for q in range(QT):
                    mm = pe.transpose(MISC[:, q * 128:(q + 1) * 128], O[:, q, :], ident)
                mm.then_inc(s["o2t"], 1)
                pe.wait_ge(s["ote"], b + 1)
                pe.matmul(MISC[:, :], wq[:, 3, :], OT[:, :], start=True, stop=True).then_inc(s["wo"], 1)
                pe.wait_ge(s["x1"], b + 1)
                for q in range(QT):
                    mm = pe.transpose(MISC[:, q * 128:(q + 1) * 128], x1T[:, q * 128:(q + 1) * 128], ident)
                mm.then_inc(s["xtr"], 1)
                pe.wait_ge(s["xte"], b + 1)
                pe.matmul(MISC[:, :], weff[:, b, :], x1T[:, :], start=True, stop=True).then_inc(s["zmm"], 1)
                pe.wait_ge(s["zte"], b + 1)
                for q in range(QT):
                    mm = pe.transpose(MISC[:, q * 128:(q + 1) * 128], zT[:, q * 128:(q + 1) * 128], ident)
                mm.then_inc(s["ztr"], 1)
                pe.wait_ge(s["zlo"], b + 1)
                for q in range(QT):
                    mm = pe.matmul(MISC[:, q * E:(q + 1) * E], zT[:, q * 128:(q + 1) * 128], col[:, WG:WG + E],
                                   start=True, stop=True)
                mm.then_inc(s["lgm"], 1)
                pe.wait_ge(s["msk"], b + 1)
                for q in range(QT):
                    t = QT * b + q
                    for p in range(t + 1):
                        mm = pe.matmul(MISC[:, 64 + q * E:64 + (q + 1) * E], ones[:, :] if p < t else tri,
                                       mask[:, p, :], start=(p == 0), stop=(p == t))
                mm.then_inc(s["cum"], 1)
                pe.wait_ge(s["dg"], QT * (b + 1))
                pe.matmul(MISC[:, :], ones[:, :], diag[:, :, :], start=True, stop=True).then_inc(s["srm"], 1)

            pe.wait_ge(s["cst"], 16)
            pe.wait_ge(s["ones"], 1)
            pe.wait_ge(s["hm"], 2 * B)
            pe.transpose(TP[0][:, 0:128], ones[:, :], ident).then_inc(s["tp"], 1)
            pe.transpose(TP[0][:, 128:256], ones[:, :], ident).then_inc(s["pv"], 1)
            for k in range(AHEAD):
                if k == 0:
                    pe.wait_ge(s["qhi"], B)
                    pe.wait_ge(s["qlo"], B)
                qh, ql = Qh[:, 0, k * 128:(k + 1) * 128], Ql[:, 0, k * 128:(k + 1) * 128]
                if k == 0:
                    pe.wait_ge(s["hi"], 1)
                    pe.wait_ge(s["lo"], 1)
                pe.matmul(SC[k][:, :], ql, Kh[:, 0, :], start=True, stop=False)
                pe.matmul(SC[k][:, :], qh, Kl[:, 0, :], start=False, stop=False)
                pe.matmul(SC[k][:, :], qh, Kh[:, 0, :], start=False, stop=True).then_inc(s["sc"], 1)
            for b in range(B):
                with pe.Fori(0, NG - 1) as g:
                    group(b, g)
                group(b, NG - 1)
                after(b)

            for h in range(2):
                for t in range(NT):
                    if h == 0:
                        pe.wait_ge(s["disp0"], t + 1)
                    pe.matmul(SC[h][:, :], Zl[:, t, :], D[:, t, 512 * h:512 * (h + 1)],
                              start=(t == 0), stop=False)
                    mm = pe.matmul(SC[h][:, :], Zh[:, t, :], D[:, t, 512 * h:512 * (h + 1)],
                                   start=False, stop=(t == NT - 1))
                mm.then_inc(s["dsp"], 1)

            def up(e):
                pe.wait_ge(s["dtea"], 1)
                pe.wait_ge(s["dted"], 1)
                if e >= 2:
                    pe.wait_ge(s[("heva", "hevd")[e % 2]], NJ * (e // 2))
                for j in range(NJ):
                    mm = pe.matmul(SC[2 + e % 2][:, j * 128:(j + 1) * 128], w1s[:, e, j * 128:(j + 1) * 128],
                                   DT[:, e * CAP:(e + 1) * CAP], start=True, stop=True)
                mm.then_inc(s["hmm"], 1)

            def down(e):
                pe.wait_ge(s[("heva", "hevd")[e % 2]], NJ * (e // 2 + 1))
                if e >= 2:
                    pe.wait_ge(s["eol"], e - 1)
                bank = TP[e % 2][:, 0:C]
                pe.matmul(bank, ones[0:1, :], b2s[0:1, e * C:(e + 1) * C], start=True, stop=False)
                for j in range(NJ):
                    mm = pe.matmul(bank, HT[e % 2][:, j, :], w2s[:, e, j, :], start=False, stop=(j == NJ - 1))
                mm.then_inc(s["eom"], 1)

            def combine(e):
                pe.wait_ge(s["eol"], e + 1)
                pe.wait_ge(s["dt2"], e + 1)
                for h, bank in enumerate((PV, MISC)):
                    pe.matmul(bank[:, :], EOl[:, e, :], D[:, e, 512 * h:512 * (h + 1)], start=(e == 0), stop=False)
                    mm = pe.matmul(bank[:, :], EOh[:, e, :], D[:, e, 512 * h:512 * (h + 1)],
                                   start=False, stop=(e == E - 1))
                    if e == E - 1:
                        mm.then_inc(s["cmb"], 1)

            pe.wait_ge(s["w1"], 16)
            pe.wait_ge(s["w2"], 16)
            pe.wait_ge(s["b2"], 16)
            pe.wait_ge(s["sre"], B)
            up(0)
            for e in range(E):
                if e + 1 < E:
                    up(e + 1)
                down(e)
                if e:
                    combine(e - 1)
            combine(E - 1)
            for h in range(2):
                pe.wait_ge(s[("ctea", "cted")[h]], 1)
                for q in range(QT):
                    t = QT * h + q
                    mm = pe.transpose(SC[h][:, q * 128:(q + 1) * 128], CT[:, t * 128:(t + 1) * 128], ident)
                mm.then_inc(s["ftr"], 1)


def kernel(**a):
    import concourse.bacc as bacc
    from concourse.bass_utils import run_bass_kernel_spmd

    a = {k: np.asarray(v) for k, v in a.items()}
    f = np.float32
    p = "L0_cond_"
    parts = [a[p + "W_up"].transpose(0, 2, 1), a[p + "W_gate"].transpose(0, 2, 1),
             a[p + "W_down"].transpose(0, 2, 1).reshape(E, 2, 128, C).transpose(0, 2, 1, 3).reshape(E, 128, 2 * C),
             a[p + "b_up"].reshape(E, 2, 128).transpose(0, 2, 1),
             a[p + "b_gate"].reshape(E, 2, 128).transpose(0, 2, 1),
             a[p + "b_down"].reshape(E, C, 1)]
    q = "L0_attn_"
    cols = [a[q + "bq"].reshape(C, 1), a[q + "bk"].reshape(C, 1), a[q + "bo"].reshape(C, 1),
            a["L0_cond2_b_base"].reshape(C, 1),
            np.repeat(a[q + "conv_w"].transpose(1, 0, 2), DH, axis=0).reshape(C, H * TAPS),
            np.repeat(a[q + "conv_b"].reshape(1, H), 128, axis=0),
            a["L0_ffn_b1"].reshape(E * NJ, 128).T, a["L0_ffn_wg"],
            np.repeat(a["cond_8"], 16, axis=1).T, np.repeat(a[q + "bv"].reshape(1, C), 128, axis=0)]
    lane = np.arange(128)
    consts = np.concatenate([
        np.eye(128), lane[:, None] <= lane[None, :],
        np.repeat((np.arange(E) + E)[None], 128, axis=0),
        lane[:, None] + CAP * np.arange(E)[None],
        np.repeat(np.arange(E * CAP)[None], 128, axis=0)], axis=1).astype(f)
    arrays = {
        "cond": a["cond_8"].reshape(1, B * E),
        "wexp": np.concatenate(parts, axis=2),
        "xT": a["x"].reshape(T, C).T,
        "wqkvo": np.stack([a[q + n].T for n in ("Wq", "Wk", "Wv", "Wo")], axis=1),
        "lora": np.stack([a["L0_cond2_As"].reshape(128, C),
                          a["L0_cond2_Bs"].transpose(0, 2, 1).reshape(128, C), a["L0_cond2_W_base"].T], axis=1),
        "cols": np.concatenate(cols, axis=1),
        "b2row": a["L0_ffn_b2"].reshape(1, E * C),
        "w1": a["L0_ffn_w1"].transpose(1, 0, 2),
        "w2": a["L0_ffn_w2"].reshape(E, NJ, 128, C).transpose(2, 0, 1, 3),
        "consts": consts,
    }
    arrays = {"in_" + k: np.ascontiguousarray(v) for k, v in arrays.items()}
    nc = bacc.Bacc("TRN2", target_bir_lowering=False, num_devices=1)
    args = [nc.dram_tensor(k, v.shape, mybir.dt.from_np(v.dtype), kind="ExternalInput").ap()
            for k, v in arrays.items()]
    out = nc.dram_tensor("out", (T, C), mybir.dt.float32, kind="ExternalOutput").ap()
    build(nc, *args, out)
    r = run_bass_kernel_spmd(nc, [arrays], core_ids=[0])
    return r.results[0]["out"].reshape(B, S, C)
```

```python
import numpy as np
import concourse.bass as bass
from concourse import mybir
from contextlib import ExitStack

B, S, C = 2, 512, 128
H, DH, TAPS = 16, 8, 3
E, HE, HID = 8, 256, 512
T = B * S
NT = T // 128
QT = S // 128
G = 4
NG = H // G
U = G * QT
RING = 8
AHEAD = 4
TURN = 5
STAGES = 10
AT_PE = {(0, 5): 0, (0, 7): 1, (0, 9): 2, (0, 11): 3, (0, 13): 4, (1, 0): 5, (NG - 1, 5): 6, (NG - 1, 8): 7}
AT_ACT = {(0, 6): 0, (0, 10): 2, (0, 14): 4, (1, 1): 5, (NG - 1, 10): 7}
AT_DVE = {(0, 8): 1, (0, 12): 3, (0, 15): 4, (1, 1): 5, (NG - 1, 6): 6, (NG - 1, 8): 8, (NG - 1, 11): 9}
CAP = T // E
VW = 32
NJ = HID // 128

BQ, BK, BO, BB, CW = 0, 1, 2, 3, 4
CB = CW + H * TAPS
B1 = CB + H
WG = B1 + E * NJ
LW = WG + E
BV = LW + B
NCOLS = BV + C
WU, WGT, WD, EB = 0, HE, 2 * HE, 2 * HE + 2 * C
EW = EB + 5
ID, TRI, IO8, IP, IOTA = 0, 128, 256, 264, 272
NCONST = IOTA + E * CAP


def build(nc, cond, wexp, xT, wqkvo, lora, cols, b2row, w1, w2, consts, out):
    f32, f32r = mybir.dt.float32, mybir.dt.float32r
    u32 = mybir.dt.uint32
    ALU, ACT, AX = mybir.AluOpType, mybir.ActivationFunctionType, mybir.AxisListType

    with ExitStack() as ctx:
        def sb(name, shape, dt=f32):
            return ctx.enter_context(nc.sbuf_tensor(name, shape, dt))

        def sem(name):
            return ctx.enter_context(nc.semaphore(name))

        banks = [ctx.enter_context(nc.psum_tensor(n, [128, 512], f32))
                 for n in ("sc0", "sc1", "sc2", "sc3", "tp0", "tp1", "pvbank", "misc")]
        SC, TP, PV, MISC = banks[0:4], banks[4:6], banks[6], banks[7]

        condS = sb("condS", [1, B * E])
        cmax = sb("cmax", [1, B * 8])
        cidx = sb("cidx", [1, B * 8], u32)
        we = sb("we", [128, B, EW])
        hb = sb("hb", [128, B, 2])
        xTs = sb("xTs", [128, T])
        wq = sb("wq", [128, 4, 128])
        lo_w = sb("lo_w", [128, 3, 128])
        bs = sb("bs", [128, B, 128])
        weff = sb("weff", [128, B, 128])
        col = sb("col", [128, NCOLS])
        b2s = sb("b2s", [1, E * C])
        w1s = sb("w1s", [128, E, HID])
        w2s = sb("w2s", [128, E, NJ, C])
        cst = sb("cst", [128, NCONST])
        ones = sb("ones", [128, 128])
        ident, tri = cst[:, ID:ID + 128], cst[:, TRI:TRI + 128]

        RAW = sb("RAW", [128, S])
        q32 = RAW
        yT = sb("yT", [128, B, S])
        Qh = sb("Qh", [128, B, S], f32r)
        Ql = sb("Ql", [128, B, S], f32r)
        Kp = sb("Kp", [128, B, S + 2])
        V = sb("V", [128, B, QT, H, DH])
        Vst = sb("Vst", [128, QT, G, VW])
        cwS = sb("cwS", [128, 2, TAPS])
        ta = sb("ta", [128, S])
        tc_ = sb("tc_", [128, S])
        td = sb("td", [128, 2, S])
        kc = sb("kc", [128, S])
        Kh = sb("Kh", [128, 2, S], f32r)
        Kl = sb("Kl", [128, 2, S], f32r)
        spare = sb("spare", [128, 4])
        nbias = sb("nbias", [128, RING])
        Pb = sb("Pb", [128, RING, S])
        PT = sb("PT", [128, G, QT, S])
        rec = sb("rec", [128, QT, G])
        O = sb("O", [128, QT, C])
        OT = sb("OT", [128, S])
        x1T, zT = yT[:, 0, :], yT[:, 1, :]
        X1 = sb("X1", [128, NT, C])
        Zh = sb("Zh", [128, NT, C], f32r)
        Zl = sb("Zl", [128, NT, C], f32r)
        lg = sb("lg", [128, QT, E])
        es = sb("es", [128, QT, E])
        eq = sb("eq", [128, QT, E])
        mask = sb("mask", [128, NT, E])
        r1 = sb("r1", [128, 8, QT])
        slot = sb("slot", [128, NT])
        gval = sb("gval", [128, NT])
        diag = OT[:, :].rearrange("p (q t) -> p q t", q=QT)
        SR = sb("SR", [128, T])
        D = sb("D", [128, NT, T], f32r)
        EOh, EOl = Zh, Zl

        flat = PT[:, :, :, :].rearrange("p g k s -> p (g k s)")
        Ub = [[flat[:, (4 * b + i) * 512:(4 * b + i + 1) * 512] for i in range(2)] for b in range(B)]
        Tb = [[flat[:, (4 * b + 2 + i) * 512:(4 * b + 3 + i) * 512] for i in range(2)] for b in range(B)]
        Sb_ = [[flat[:, 4096 + (4 * b + i) * 512:4096 + (4 * b + i + 1) * 512] for i in range(2)] for b in range(B)]
        Hb = [[flat[:, 4096 + (4 * b + 2 + i) * 512:4096 + (4 * b + 3 + i) * 512] for i in range(2)] for b in range(B)]
        DT = flat[:, 0:1024]
        HT = [flat[:, 1024 + 512 * i:1536 + 512 * i].rearrange("p (j s) -> p j s", j=NJ) for i in range(2)]
        CT = flat[:, 2048:3072]
        OUT = flat[:, 3072:4096].rearrange("p (t m) -> p t m", t=NT)

        names = """spare cond cmax cidx we0 we1 xt wq lora cols b2 w1 w2 cst outd
            hb bsc ones kpad vpad wefmm wefe
            mlp ut sm hm ymm yev qmm kmm vmm qev qhi qlo kev vev
            cw ac d kc hi lo sc mx ex tp evd eva vst pv raw
            otr rcp on o2t ote wo x1 xtr xte zmm zte ztr zhi zlo lgm nl nla esr nr msk cum rt
            slt dg srm sre disp0 dsp dtea dted hmm heva hevd eom eoh eol dt2 cmb ctea cted ftr fo""".split()
        s = {n: sem("s_" + n) for n in names}

        block = ctx.enter_context(nc.Block())

        @block.sync
        def _(sp):
            sp.dma_start(condS[:, :], cond).then_inc(s["cond"], 16)
            sp.dma_start(xTs[:, :], xT).then_inc(s["xt"], 16)
            sp.wait_ge(s["cidx"], B)
            for b in range(B):
                e = sp.value_load(cidx[0:1, 8 * b:8 * b + 1], min_val=0, max_val=E - 1)
                sp.dma_start(we[:, b:b + 1, :], wexp[bass.ds(e, 1), :, :].rearrange("e p n -> p e n"))\
                    .then_inc(s[f"we{b}"], 16)
            sp.dma_start(w1s[:, :, :], w1).then_inc(s["w1"], 16)
            sp.dma_start(w2s[:, :, :, :], w2).then_inc(s["w2"], 16)
            sp.dma_start(b2s[:, :], b2row).then_inc(s["b2"], 16)
            for t in range(NT):
                sp.wait_ge(s["fo"], t + 1)
                sp.dma_start(out[t * 128:(t + 1) * 128, :], OUT[:, t, :]).then_inc(s["outd"], 16)
            sp.wait_ge(s["outd"], 16 * NT)

        @block.gpsimd
        def _(pool):
            pool.memset(ones[:, :], 1.0).then_inc(s["ones"], 1)
            for b in range(B):
                pool.memset(Kp[:, b, 0:1], 0.0).then_inc(s["kpad"], 1)
                pool.memset(Kp[:, b, S + 1:S + 2], 0.0).then_inc(s["kpad"], 1)
            pool.memset(Vst[:, :, :, DH:DH + 1], 1.0).then_inc(s["vpad"], 1)
            pool.memset(Vst[:, :, :, DH + 1:VW], 0.0).then_inc(s["vpad"], 1)
            pool.wait_ge(s["cols"], 16)

            def fetch_taps(hd, o, n):
                src = col[:, CW + TAPS * o:CW + TAPS * (o + 1)] if isinstance(o, int) else \
                    col[:, bass.ds(CW + TAPS * o, TAPS)]
                pool.wait_ge(s["d"], hd)
                pool.tensor_copy(cwS[:, n, :], src).then_inc(s["cw"], 1)

            def low_half(hd, n):
                pool.wait_ge(s["cw"], hd + 3)
                pool.wait_ge(s["hi"], hd + 1)
                pool.tensor_tensor(Kl[:, n, :], kc[:, :], Kh[:, n, :].bitcast(f32), ALU.subtract)\
                    .then_inc(s["lo"], 1)

            def outer_taps(hd, b, n):
                pool.tensor_scalar(ta[:, :], Kp[:, b, 0:S], cwS[:, n, 0:1], 1.0, ALU.mult, ALU.mult)\
                    .then_inc(s["ac"], 1)
                pool.tensor_scalar(tc_[:, :], Kp[:, b, 2:S + 2], cwS[:, n, 2:3], 1.0, ALU.mult, ALU.mult)\
                    .then_inc(s["ac"], 1)
                pool.wait_ge(s["ac"], 2 * hd + 2)
                if not isinstance(hd, int) or hd >= 2:
                    pool.wait_ge(s["kc"], hd - 1)
                pool.tensor_tensor(td[:, n, :], ta[:, :], tc_[:, :], ALU.add).then_inc(s["d"], 1)

            pool.wait_ge(s["kpad"], 2 * B)
            pool.wait_ge(s["kev"], 1)
            for hd in range(2):
                fetch_taps(hd, hd, hd)
                pool.wait_ge(s["cw"], hd + 1)
                outer_taps(hd, 0, hd)
            for hd in range(2):
                fetch_taps(hd + 2, hd + 2, hd)
                low_half(hd, hd)
                outer_taps(hd + 2, 0, hd)
            pool.wait_ge(s["kev"], 2)

            def group(b, g):
                for j in range(G):
                    hd = H * b + G * g + j
                    o = G * g + j + 4
                    over = isinstance(g, int) and o >= H
                    if isinstance(g, int) and hd + 4 >= B * H:
                        if hd + 2 < B * H:
                            pool.wait_ge(s["hi"], hd + 3)
                            pool.tensor_tensor(Kl[:, j % 2, :], kc[:, :], Kh[:, j % 2, :].bitcast(f32),
                                               ALU.subtract).then_inc(s["lo"], 1)
                        continue
                    fetch_taps(hd + 4, o - H if over else o, j % 2)
                    low_half(hd + 2, j % 2)
                    outer_taps(hd + 4, b + 1 if over else b, j % 2)

            for b in range(B):
                with pool.Fori(0, NG - 1) as g:
                    group(b, g)
                group(b, NG - 1)

        @block.scalar
        def _(act):
            act.dma_start(col[:, :], cols).then_inc(s["cols"], 16)
            act.dma_start(wq[:, :, :], wqkvo).then_inc(s["wq"], 16)
            act.dma_start(lo_w[:, :, :], lora).then_inc(s["lora"], 16)
            act.dma_start(cst[:, :], consts).then_inc(s["cst"], 16)

            def high_first(hd):
                act.wait_ge(s["kc"], hd + 1)
                act.activation(Kh[:, hd, :], kc[:, :], ACT.Copy).then_inc(s["hi"], 1)

            act.wait_ge(s["spare"], 1)
            act.activation(spare[:, 2:3], spare[:, 0:1], ACT.Copy).then_inc(s["ex"], 1)
            act.activation(spare[:, 3:4], spare[:, 1:2], ACT.Copy).then_inc(s["eva"], 1)

            for b in range(B):
                act.wait_ge(s["hb"], b + 1)
                for i in range(2):
                    act.wait_ge(s["mlp"], 4 * b + i + 1)
                    act.activation(Ub[b][i], SC[i][:, :], ACT.Identity, bias=hb[:, b, i:i + 1], scale=0.5)\
                        .then_inc(s["ut"], 1)
                    act.activation(Tb[b][i], SC[i][:, :], ACT.Tanh, bias=hb[:, b, i:i + 1], scale=0.5)\
                        .then_inc(s["ut"], 1)
                if b == 1:
                    high_first(0)
                act.wait_ge(s["kmm"], b + 1)
                act.activation(Kp[:, b, 1:S + 1], PV[:, :], ACT.Identity, bias=col[:, BK:BK + 1])\
                    .then_inc(s["kev"], 1)
                act.wait_ge(s["qev"], b + 1)
                act.activation(Qh[:, b, :], q32[:, :], ACT.Copy).then_inc(s["qhi"], 1)
            high_first(1)

            def high_half(hd, n):
                act.wait_ge(s["kc"], hd + 1)
                act.wait_ge(s["sc"], QT * (hd - 1))
                act.activation(Kh[:, n, :], kc[:, :], ACT.Copy).then_inc(s["hi"], 1)

            def exp(n, k):
                act.wait_ge(s["mx"], n + 2)
                act.activation(Pb[:, k, :], Pb[:, k, :], ACT.Exp, bias=nbias[:, k:k + 1], scale=-1.0)\
                    .then_inc(s["ex"], 1)

            def stage_values(b, g):
                act.wait_ge(s["pv"], H * b + G * g + 1)
                src = V[:, b, :, bass.ds(G * g, G), :] if not isinstance(g, int) else \
                    V[:, b, :, G * g:G * g + G, :]
                act.activation(Vst[:, :, :, 0:DH], src, ACT.Copy).then_inc(s["vst"], 1)

            def after(b, k):
                tiles = slice(QT * b, QT * (b + 1))
                by_token = MISC[:, :].rearrange("p (t m) -> p t m", t=QT)
                if k == 0:
                    act.wait_ge(s["o2t"], b + 1)
                    act.activation(OT[:, :], MISC[:, :], ACT.Copy).then_inc(s["ote"], 1)
                elif k == 2:
                    act.wait_ge(s["xtr"], b + 1)
                    act.activation(X1[:, tiles, :], by_token, ACT.Copy).then_inc(s["xte"], 1)
                elif k == 4:
                    act.wait_ge(s["ztr"], b + 1)
                    act.activation(Zh[:, tiles, :], by_token, ACT.Copy).then_inc(s["zhi"], 1)
                elif k == 5:
                    act.wait_ge(s["nl"], b + 1)
                    act.activation(es[:, :, :], lg[:, :, :], ACT.Exp).then_inc(s["nla"], 1)
                elif k == 7:
                    act.wait_ge(s["srm"], b + 1)
                    act.activation(SR[:, S * b:S * (b + 1)], MISC[:, :], ACT.Copy).then_inc(s["sre"], 1)

            def unit(b, g, u):
                n = U * (NG * b + g) + u
                hd = H * b + G * g + u // QT
                if b == 1 and isinstance(g, int):
                    after(0, AT_ACT.get((g, u)))
                if u % 2 == 1:
                    act.wait_ge(s["tp"], n + 2)
                    act.activation(PT[:, u // QT % G, :, (u % QT) * 128:(u % QT + 1) * 128],
                                   TP[1][:, :].rearrange("p (k q) -> p k q", k=QT), ACT.Copy)\
                        .then_inc(s["eva"], 1)
                if not isinstance(g, int) or n + AHEAD < U * NG * B:
                    exp(n + AHEAD, (u + AHEAD) % RING)
                if u % QT == 0 and (not isinstance(g, int) or hd + 2 < B * H):
                    high_half(hd + 2, (u // QT) % 2)
                if u == 3:
                    stage_values(b, g)

            act.wait_ge(s["vev"], B)
            act.wait_ge(s["vpad"], 2)
            for k in range(AHEAD):
                exp(k, k)
            for u in range(TURN):
                unit(0, 0, u)
            with act.Fori(0, NG - 1) as g:
                for u in range(TURN, U + TURN):
                    unit(0, g + u // U, u % U)
            for u in range(TURN, U):
                unit(0, NG - 1, u)
            for u in range(U + TURN):
                unit(1, u // U, u % U)
            with act.Fori(1, NG - 1) as g:
                for u in range(TURN, U + TURN):
                    unit(1, g + u // U, u % U)
            for u in range(TURN, U):
                unit(1, NG - 1, u)
            for k in range(STAGES):
                after(1, k)

            act.wait_ge(s["dsp"], 1)
            act.activation(DT[:, 0:512], SC[0][:, :], ACT.Copy).then_inc(s["dtea"], 1)
            for e in range(E):
                if e % 2 == 0:
                    act.wait_ge(s["hmm"], e + 1)
                    if e >= 2:
                        act.wait_ge(s["eom"], e - 1)
                    for j in range(NJ):
                        act.activation(HT[0][:, j, :], SC[2][:, j * 128:(j + 1) * 128], ACT.Relu,
                                       bias=col[:, B1 + NJ * e + j:B1 + NJ * e + j + 1]).then_inc(s["heva"], 1)
                act.wait_ge(s["eom"], e + 1)
                act.activation(EOh[:, e, :], TP[e % 2][:, 0:C], ACT.Copy).then_inc(s["eoh"], 1)
            act.wait_ge(s["cmb"], 1)
            act.activation(CT[:, 0:512], PV[:, :], ACT.Copy).then_inc(s["ctea"], 1)

        @block.vector
        def _(dve):
            dve.memset(nbias[:, 0:1], 0.0).then_inc(s["evd"], 1)
            dve.memset(nbias[:, 1:2], 0.0).then_inc(s["raw"], 1)
            dve.memset(nbias[:, 2:3], 0.0).then_inc(s["mx"], 1)
            dve.memset(nbias[:, 3:4], 0.0).then_inc(s["on"], 1)
            dve.memset(spare[:, 0:2], 0.0).then_inc(s["spare"], 1)
            dve.wait_ge(s["cond"], 16)
            for b in range(B):
                dve.max(cmax[:, 8 * b:8 * b + 8], condS[:, E * b:E * b + E]).then_inc(s["cmax"], 1)
            for b in range(B):
                dve.wait_ge(s["cmax"], b + 1)
                dve.max_index(cidx[:, 8 * b:8 * b + 8], cmax[:, 8 * b:8 * b + 8],
                              condS[:, E * b:E * b + E]).then_inc(s["cidx"], 1)
            dve.wait_ge(s["lora"], 16)
            dve.wait_ge(s["cols"], 16)
            for b in range(B):
                dve.tensor_scalar(bs[:, b, :], lo_w[:, 1, :], col[:, LW + b:LW + b + 1], 2.0,
                                  ALU.mult, ALU.mult).then_inc(s["bsc"], 1)
            for b in range(B):
                dve.wait_ge(s[f"we{b}"], 16)
                dve.tensor_scalar(hb[:, b, :], we[:, b, EB:EB + 2], 0.5, None, ALU.mult).then_inc(s["hb"], 1)
            for b in range(B):
                dve.wait_ge(s["wefmm"], b + 1)
                dve.tensor_tensor(weff[:, b, :], MISC[:, 0:C], lo_w[:, 2, :], ALU.add).then_inc(s["wefe"], 1)
            def middle_tap(hd, b, o, n):
                at = CW + TAPS * o + 1
                w = col[:, at:at + 1] if isinstance(o, int) else col[:, bass.ds(at, 1)]
                dve.wait_ge(s["d"], hd + 1)
                dve.wait_ge(s["lo"], hd)
                dve.scalar_tensor_tensor(kc[:, :], Kp[:, b, 1:S + 1], w, td[:, n, :], ALU.mult, ALU.add)\
                    .then_inc(s["kc"], 1)

            for b in range(B):
                for i in range(2):
                    dve.wait_ge(s["ut"], 4 * b + 2 * i + 2)
                    dve.scalar_tensor_tensor(Sb_[b][i], Tb[b][i], 1.0, Ub[b][i], ALU.add, ALU.mult)\
                        .then_inc(s["sm"], 1)
                if b == 1:
                    middle_tap(0, 0, 0, 0)
                for i in range(2):
                    dve.wait_ge(s["sm"], 2 * b + i + 1)
                    dve.wait_ge(s["mlp"], 4 * b + 3 + i)
                    dve.scalar_tensor_tensor(Hb[b][i], SC[2 + i][:, :], we[:, b, EB + 2 + i:EB + 3 + i],
                                             Sb_[b][i], ALU.add, ALU.mult).then_inc(s["hm"], 1)
                dve.wait_ge(s["ymm"], b + 1)
                dve.tensor_scalar(yT[:, b, :], TP[0][:, :], we[:, b, EB + 4:EB + 5], None, ALU.add)\
                    .then_inc(s["yev"], 1)
                dve.wait_ge(s["qmm"], b + 1)
                if b:
                    dve.wait_ge(s["qhi"], b)
                    dve.wait_ge(s["qlo"], b)
                dve.tensor_scalar(q32[:, :], TP[1][:, :], col[:, BQ:BQ + 1], -float(DH) ** -0.5,
                                  ALU.add, ALU.mult).then_inc(s["qev"], 1)
                dve.wait_ge(s["vmm"], b + 1)
                bv = col[:, BV:BV + C].rearrange("p (h d) -> p h d", d=DH)
                for k in range(QT):
                    v = dve.tensor_tensor(V[:, b, k, :, :], MISC[:, k * 128:(k + 1) * 128]
                                          .rearrange("p (h d) -> p h d", d=DH), bv, ALU.add)
                v.then_inc(s["vev"], 1)
                dve.wait_ge(s["qhi"], b + 1)
                dve.tensor_tensor(Ql[:, b, :], q32[:, :], Qh[:, b, :].bitcast(f32), ALU.subtract)\
                    .then_inc(s["qlo"], 1)

            def maximum(n, k, o):
                cb = col[:, CB + o:CB + o + 1] if isinstance(o, int) else col[:, bass.ds(CB + o, 1)]
                dve.wait_ge(s["sc"], n + 1)
                dve.tensor_scalar(Pb[:, k, :], SC[k % 4][:, :], cb, None, ALU.subtract, ALU.min,
                                  accum_out=nbias[:, k:k + 1]).then_inc(s["mx"], 1)

            def raw_out(b, g):
                dve.wait_ge(s["pv"], H * b + G * g + 1)
                dve.wait_ge(s["otr"], NG * b + g)
                dve.tensor_copy(RAW[:, :], PV[:, :]).then_inc(s["raw"], 1)

            def normalise(b, g):
                dve.wait_ge(s["otr"], NG * b + g + 1)
                t = MISC[:, :].rearrange("p (j t w) -> p t j w", j=G, t=QT)
                dve.reciprocal(rec[:, :, :], t[:, :, :, DH]).then_inc(s["rcp"], 1)
                dve.wait_ge(s["rcp"], NG * b + g)
                r = rec[:, :, :].rearrange("p t (j a) -> p t j a", a=1)
                if isinstance(g, int):
                    at = (g - 1) % NG * G * DH
                    dst = O[:, :, at:at + G * DH]
                else:
                    dst = O[:, :, bass.ds(G * DH * (g - 1), G * DH)]
                dve.tensor_tensor(dst.rearrange("p t (j d) -> p t j d", d=DH),
                                  t[:, :, :, 0:DH], r.broadcast_to([128, QT, G, DH]), ALU.mult)\
                    .then_inc(s["on"], 1)

            def over_experts(a):
                return a.rearrange("p (t a) -> p t a", a=1).broadcast_to([128, QT, E])

            io8 = cst[:, IO8:IO8 + E].rearrange("p (a e) -> p a e", a=1).broadcast_to([128, QT, E])
            lmax, ssum, rs, gmax, idx, pos, keep, s1 = (r1[:, i, :] for i in range(8))

            def after(b, k):
                tiles = slice(QT * b, QT * (b + 1))
                n = [14 * b + (9 if k == 6 else 0)]

                def step(ins):
                    n[0] += 1
                    ins.then_inc(s["nr"], 1)
                    dve.wait_ge(s["nr"], n[0])

                if k == 1:
                    dve.wait_ge(s["wo"], b + 1)
                    dve.scalar_tensor_tensor(x1T, MISC[:, :], col[:, BO:BO + 1], xTs[:, S * b:S * (b + 1)],
                                             ALU.add, ALU.add).then_inc(s["x1"], 1)
                elif k == 3:
                    dve.wait_ge(s["zmm"], b + 1)
                    dve.tensor_scalar(zT, MISC[:, :], col[:, BB:BB + 1], None, ALU.add).then_inc(s["zte"], 1)
                elif k == 4:
                    dve.wait_ge(s["zhi"], b + 1)
                    dve.tensor_tensor(Zl[:, tiles, :], MISC[:, :].rearrange("p (t m) -> p t m", t=QT),
                                      Zh[:, tiles, :].bitcast(f32), ALU.subtract).then_inc(s["zlo"], 1)
                elif k == 5:
                    L = MISC[:, 0:QT * E].rearrange("p (t e) -> p t e", e=E)
                    dve.wait_ge(s["lgm"], b + 1)
                    step(dve.tensor_reduce(lmax, L, AX.X, ALU.max))
                    dve.tensor_tensor(lg[:, :, :], L, over_experts(lmax), ALU.subtract).then_inc(s["nl"], 1)
                    dve.wait_ge(s["nla"], b + 1)
                    step(dve.tensor_reduce(ssum, es[:, :, :], AX.X, ALU.add))
                    step(dve.reciprocal(rs, ssum))
                    step(dve.tensor_tensor(es[:, :, :], es[:, :, :], over_experts(rs), ALU.mult))
                    step(dve.tensor_reduce(gmax, es[:, :, :], AX.X, ALU.max))
                    step(dve.tensor_tensor(eq[:, :, :], es[:, :, :], over_experts(gmax), ALU.is_equal))
                    step(dve.scalar_tensor_tensor(eq[:, :, :], eq[:, :, :], -float(E), io8, ALU.mult, ALU.add))
                    step(dve.tensor_reduce(idx, eq[:, :, :], AX.X, ALU.min))
                    step(dve.tensor_scalar(s1, idx, float(E), None, ALU.add))
                    dve.tensor_tensor(mask[:, tiles, :], io8, over_experts(s1), ALU.is_equal).then_inc(s["msk"], 1)
                elif k == 6:
                    dve.wait_ge(s["cum"], b + 1)
                    cum = MISC[:, 64:64 + QT * E].rearrange("p (t e) -> p t e", e=E)
                    step(dve.tensor_tensor(eq[:, :, :], cum, mask[:, tiles, :], ALU.mult))
                    step(dve.tensor_reduce(pos, eq[:, :, :], AX.X, ALU.add))
                    step(dve.tensor_scalar(keep, pos, float(CAP), None, ALU.is_le))
                    dve.tensor_tensor(gval[:, tiles], gmax, keep, ALU.mult).then_inc(s["rt"], 1)
                    step(dve.scalar_tensor_tensor(s1, idx, float(CAP), pos, ALU.mult, ALU.add))
                    step(dve.tensor_tensor(s1, s1, keep, ALU.mult))
                    dve.tensor_scalar(slot[:, tiles], s1, -1.0, None, ALU.add).then_inc(s["slt"], 1)
                    dve.wait_ge(s["slt"], b + 1)
                    for q in range(QT):
                        dve.tensor_scalar(diag[:, q, :], ident, slot[:, QT * b + q:QT * b + q + 1], None, ALU.mult)\
                            .then_inc(s["dg"], 1)
                elif k in (8, 9):
                    for t in range(QT * b + 2 * (k - 8), QT * b + 2 * (k - 7)):
                        dve.tensor_scalar(D[:, t, :], cst[:, IOTA:IOTA + T], slot[:, t:t + 1], None, ALU.is_equal)\
                            .then_inc(s["disp0"], 1)

            def unit(b, g, u):
                n = U * (NG * b + g) + u
                m, j = u + AHEAD, u // QT
                if not (isinstance(g, int) and b + g == 0):
                    if u == 2:
                        raw_out(b, g)
                    elif u == 4:
                        normalise(b, g)
                if b == 1 and isinstance(g, int):
                    after(0, AT_DVE.get((g, u)))
                if not isinstance(g, int) or n + AHEAD < U * NG * B:
                    over = isinstance(g, int) and G * g + m // QT >= H
                    maximum(n + AHEAD, m % RING, G * g + m // QT - (H if over else 0))
                if u % 2 == 0:
                    dve.wait_ge(s["tp"], n + 2)
                    dve.tensor_copy(PT[:, j % G, :, (u % QT) * 128:(u % QT + 1) * 128],
                                    TP[0][:, :].rearrange("p (k q) -> p k q", k=QT))\
                        .then_inc(s["evd"], 1)
                if u % QT == 2 and (not isinstance(g, int) or H * b + G * g + j + 3 < B * H):
                    over = isinstance(g, int) and G * g + j + 3 >= H
                    middle_tap(H * b + G * g + j + 3, b + 1 if over else b,
                               G * g + j + 3 - (H if over else 0), (j + 1) % 2)

            middle_tap(1, 0, 1, 1)
            for k in range(AHEAD):
                maximum(k, k, 0)
            middle_tap(2, 0, 2, 0)
            for u in range(TURN):
                unit(0, 0, u)
            with dve.Fori(0, NG - 1) as g:
                for u in range(TURN, U + TURN):
                    unit(0, g + u // U, u % U)
            for u in range(TURN, U):
                unit(0, NG - 1, u)
            dve.wait_ge(s["cst"], 16)
            for u in range(U + TURN):
                unit(1, u // U, u % U)
            with dve.Fori(1, NG - 1) as g:
                for u in range(TURN, U + TURN):
                    unit(1, g + u // U, u % U)
            for u in range(TURN, U):
                unit(1, NG - 1, u)
            raw_out(1, NG)
            normalise(1, NG)
            for k in range(STAGES):
                after(1, k)

            dve.wait_ge(s["dsp"], 2)
            dve.tensor_copy(DT[:, 512:1024], SC[1][:, :]).then_inc(s["dted"], 1)
            dve.wait_ge(s["sre"], B)

            def spread(e):
                dve.tensor_scalar(D[:, e, :], SR[:, :], cst[:, IP + e:IP + e + 1], None, ALU.is_equal)\
                    .then_inc(s["dt2"], 1)

            for e in range(E):
                if e % 2 == 1:
                    dve.wait_ge(s["hmm"], e + 1)
                    if e >= 3:
                        dve.wait_ge(s["eom"], e - 1)
                    for j in range(NJ):
                        dve.tensor_scalar(HT[1][:, j, :], SC[3][:, j * 128:(j + 1) * 128],
                                          col[:, B1 + NJ * e + j:B1 + NJ * e + j + 1], 0.0, ALU.add, ALU.max)\
                            .then_inc(s["hevd"], 1)
                spread(e)
                dve.wait_ge(s["eoh"], e + 1)
                dve.tensor_tensor(EOl[:, e, :], TP[e % 2][:, 0:C], EOh[:, e, :].bitcast(f32), ALU.subtract)\
                    .then_inc(s["eol"], 1)
            dve.wait_ge(s["cmb"], 2)
            dve.tensor_copy(CT[:, 512:1024], MISC[:, :]).then_inc(s["cted"], 1)
            for t in range(NT):
                dve.wait_ge(s["ftr"], t // QT + 1)
                bank = SC[t // QT]
                dve.scalar_tensor_tensor(OUT[:, t, :], bank[:, (t % QT) * 128:(t % QT + 1) * 128],
                                         gval[:, t:t + 1], X1[:, t, :], ALU.mult, ALU.add).then_inc(s["fo"], 1)

        @block.tensor
        def _(pe):
            pe.wait_ge(s["lora"], 16)
            for b in range(B):
                pe.wait_ge(s["bsc"], b + 1)
                if b:
                    pe.wait_ge(s["wefe"], b)
                pe.matmul(MISC[:, 0:C], lo_w[:, 0, :], bs[:, b, :], start=True, stop=True).then_inc(s["wefmm"], 1)
            pe.wait_ge(s["xt"], 16)
            pe.wait_ge(s["wq"], 16)
            for b in range(B):
                x = xTs[:, S * b:S * (b + 1)]
                pe.wait_ge(s[f"we{b}"], 16)
                for i in range(4):
                    if b:
                        if i < 2:
                            pe.wait_ge(s["ut"], 4 * (b - 1) + 2 * i + 2)
                        else:
                            pe.wait_ge(s["hm"], 2 * (b - 1) + i - 1)
                    pe.matmul(SC[i][:, :], we[:, b, i * 128:(i + 1) * 128], x, start=True, stop=True)\
                        .then_inc(s["mlp"], 1)
                if b:
                    pe.wait_ge(s["yev"], b)
                for i in range(2):
                    pe.wait_ge(s["hm"], 2 * b + i + 1)
                    mm = pe.matmul(TP[0][:, :], we[:, b, WD + i * C:WD + (i + 1) * C], Hb[b][i],
                                   start=(i == 0), stop=(i == 1))
                mm.then_inc(s["ymm"], 1)
                pe.wait_ge(s["yev"], b + 1)
                if b:
                    pe.wait_ge(s["kev"], b)
                pe.matmul(PV[:, :], wq[:, 1, :], yT[:, b, :], start=True, stop=True).then_inc(s["kmm"], 1)
                if b:
                    pe.wait_ge(s["qev"], b)
                pe.matmul(TP[1][:, :], wq[:, 0, :], yT[:, b, :], start=True, stop=True).then_inc(s["qmm"], 1)
                if b == 0:
                    pe.wait_ge(s["wefe"], B)
                else:
                    pe.wait_ge(s["vev"], b)
                for k in range(QT):
                    mm = pe.matmul(MISC[:, k * 128:(k + 1) * 128], yT[:, b, k * 128:(k + 1) * 128], wq[:, 2, :],
                                   start=True, stop=True)
                mm.then_inc(s["vmm"], 1)

            def scores(n, hd, b, u):
                k, q = u % 4, u % QT
                qh, ql = Qh[:, b, q * 128:(q + 1) * 128], Ql[:, b, q * 128:(q + 1) * 128]
                h2 = (u // QT) % 2
                if q == 0:
                    pe.wait_ge(s["hi"], hd + 1)
                    pe.wait_ge(s["lo"], hd + 1)
                pe.wait_ge(s["mx"], n - 2)
                pe.matmul(SC[k][:, :], ql, Kh[:, h2, :], start=True, stop=False)
                pe.matmul(SC[k][:, :], qh, Kl[:, h2, :], start=False, stop=False)
                pe.matmul(SC[k][:, :], qh, Kh[:, h2, :], start=False, stop=True).then_inc(s["sc"], 1)

            def outputs(hd, j, gi):
                pe.wait_ge(s["evd"], 2 * hd + 3)
                pe.wait_ge(s["eva"], 2 * hd + 3)
                if j == 0:
                    pe.wait_ge(s["vst"], gi + 1)
                    pe.wait_ge(s["raw"], gi + 1)
                for k in range(QT):
                    for t in range(QT):
                        mm = pe.matmul(PV[32 * t:32 * t + VW, 128 * j:128 * (j + 1)], Vst[:, k, j, :],
                                       PT[:, j, k, 128 * t:128 * (t + 1)], start=(k == 0), stop=(k == QT - 1))
                mm.then_inc(s["pv"], 1)

            def turn(src, name):
                for q in range(QT):
                    mm = pe.transpose(MISC[:, q * 128:(q + 1) * 128], src(q), ident)
                mm.then_inc(s[name], 1)

            def by_token(b, g):
                pe.wait_ge(s["on"], NG * b + g)
                if b and not isinstance(g, int):
                    pe.wait_ge(s["nl"], 1)
                elif b and g:
                    pe.wait_ge(s["sre" if g == NG else "nl"], 1)
                pe.wait_ge(s["raw"], NG * b + g + 1)
                turn(lambda j: RAW[:, j * 128:(j + 1) * 128], "otr")

            def after(b, k):
                if k == 0:
                    pe.wait_ge(s["on"], NG * (b + 1) + 1)
                    turn(lambda q: O[:, q, :], "o2t")
                elif k == 1:
                    pe.wait_ge(s["ote"], b + 1)
                    pe.matmul(MISC[:, :], wq[:, 3, :], OT[:, :], start=True, stop=True).then_inc(s["wo"], 1)
                elif k == 2:
                    pe.wait_ge(s["x1"], b + 1)
                    turn(lambda q: x1T[:, q * 128:(q + 1) * 128], "xtr")
                elif k == 3:
                    pe.wait_ge(s["xte"], b + 1)
                    pe.matmul(MISC[:, :], weff[:, b, :], x1T, start=True, stop=True).then_inc(s["zmm"], 1)
                elif k == 4:
                    pe.wait_ge(s["zte"], b + 1)
                    turn(lambda q: zT[:, q * 128:(q + 1) * 128], "ztr")
                elif k == 5:
                    pe.wait_ge(s["zlo"], b + 1)
                    for q in range(QT):
                        mm = pe.matmul(MISC[:, q * E:(q + 1) * E], zT[:, q * 128:(q + 1) * 128],
                                       col[:, WG:WG + E], start=True, stop=True)
                    mm.then_inc(s["lgm"], 1)
                elif k == 6:
                    pe.wait_ge(s["msk"], b + 1)
                    if b == 0:
                        pe.wait_ge(s["on"], 2 * NG)
                    for q in range(QT):
                        t = QT * b + q
                        for p in range(t + 1):
                            mm = pe.matmul(MISC[:, 64 + q * E:64 + (q + 1) * E], ones[:, :] if p < t else tri,
                                           mask[:, p, :], start=(p == 0), stop=(p == t))
                    mm.then_inc(s["cum"], 1)
                elif k == 7:
                    pe.wait_ge(s["dg"], QT * (b + 1))
                    pe.matmul(MISC[:, :], ones[:, :], diag, start=True, stop=True).then_inc(s["srm"], 1)

            def unit(b, g, u):
                gi = NG * b + g
                n, m = U * gi + u, u + AHEAD
                if not isinstance(g, int) or n + AHEAD < U * NG * B:
                    over = isinstance(g, int) and G * g + m // QT >= H
                    scores(n + AHEAD, H * b + G * g + m // QT, b + 1 if over else b, m)
                pe.wait_ge(s["ex"], n + 2)
                pe.wait_ge(s["evd" if u % 2 == 0 else "eva"], (U // 2) * gi + u // 2 + 1)
                for k in range(QT):
                    mm = pe.transpose(TP[u % 2][:, k * 128:(k + 1) * 128],
                                      Pb[:, u % RING, k * 128:(k + 1) * 128], ident)
                mm.then_inc(s["tp"], 1)
                if u % QT == 1 and not (isinstance(g, int) and b + g == 0 and u == 1):
                    outputs(H * b + G * g + u // QT - 1, (u // QT - 1) % G, gi - (1 if u == 1 else 0))
                if u == 3 and not (isinstance(g, int) and b + g == 0):
                    by_token(b, g)
                if b == 1 and isinstance(g, int):
                    after(0, AT_PE.get((g, u)))

            pe.wait_ge(s["cst"], 16)
            pe.wait_ge(s["ones"], 1)
            pe.wait_ge(s["hm"], 2 * B)
            pe.transpose(TP[0][:, 0:128], ones[:, :], ident).then_inc(s["tp"], 1)
            pe.transpose(TP[0][:, 128:256], ones[:, :], ident).then_inc(s["pv"], 1)
            pe.transpose(TP[0][:, 256:384], ones[:, :], ident).then_inc(s["otr"], 1)
            for k in range(AHEAD):
                if k == 0:
                    pe.wait_ge(s["qhi"], B)
                    pe.wait_ge(s["qlo"], B)
                qh, ql = Qh[:, 0, k * 128:(k + 1) * 128], Ql[:, 0, k * 128:(k + 1) * 128]
                if k == 0:
                    pe.wait_ge(s["hi"], 1)
                    pe.wait_ge(s["lo"], 1)
                pe.matmul(SC[k][:, :], ql, Kh[:, 0, :], start=True, stop=False)
                pe.matmul(SC[k][:, :], qh, Kl[:, 0, :], start=False, stop=False)
                pe.matmul(SC[k][:, :], qh, Kh[:, 0, :], start=False, stop=True).then_inc(s["sc"], 1)
            for u in range(TURN):
                unit(0, 0, u)
            with pe.Fori(0, NG - 1) as g:
                for u in range(TURN, U + TURN):
                    unit(0, g + u // U, u % U)
            for u in range(TURN, U):
                unit(0, NG - 1, u)
            for u in range(U + TURN):
                unit(1, u // U, u % U)
            with pe.Fori(1, NG - 1) as g:
                for u in range(TURN, U + TURN):
                    unit(1, g + u // U, u % U)
            for u in range(TURN, U):
                unit(1, NG - 1, u)
            outputs(B * H - 1, G - 1, B * NG - 1)
            by_token(1, NG)
            for k in range(STAGES):
                after(1, k)

            for h in range(2):
                for t in range(NT):
                    if h == 0:
                        pe.wait_ge(s["disp0"], t + 1)
                    pe.matmul(SC[h][:, :], Zl[:, t, :], D[:, t, 512 * h:512 * (h + 1)],
                              start=(t == 0), stop=False)
                    mm = pe.matmul(SC[h][:, :], Zh[:, t, :], D[:, t, 512 * h:512 * (h + 1)],
                                   start=False, stop=(t == NT - 1))
                mm.then_inc(s["dsp"], 1)

            def up(e):
                pe.wait_ge(s["dtea"], 1)
                pe.wait_ge(s["dted"], 1)
                if e >= 2:
                    pe.wait_ge(s[("heva", "hevd")[e % 2]], NJ * (e // 2))
                for j in range(NJ):
                    mm = pe.matmul(SC[2 + e % 2][:, j * 128:(j + 1) * 128], w1s[:, e, j * 128:(j + 1) * 128],
                                   DT[:, e * CAP:(e + 1) * CAP], start=True, stop=True)
                mm.then_inc(s["hmm"], 1)

            def down(e):
                pe.wait_ge(s[("heva", "hevd")[e % 2]], NJ * (e // 2 + 1))
                if e >= 2:
                    pe.wait_ge(s["eol"], e - 1)
                bank = TP[e % 2][:, 0:C]
                pe.matmul(bank, ones[0:1, :], b2s[0:1, e * C:(e + 1) * C], start=True, stop=False)
                for j in range(NJ):
                    mm = pe.matmul(bank, HT[e % 2][:, j, :], w2s[:, e, j, :], start=False, stop=(j == NJ - 1))
                mm.then_inc(s["eom"], 1)

            def combine(e):
                pe.wait_ge(s["eol"], e + 1)
                pe.wait_ge(s["dt2"], e + 1)
                for h, bank in enumerate((PV, MISC)):
                    pe.matmul(bank[:, :], EOl[:, e, :], D[:, e, 512 * h:512 * (h + 1)], start=(e == 0), stop=False)
                    mm = pe.matmul(bank[:, :], EOh[:, e, :], D[:, e, 512 * h:512 * (h + 1)],
                                   start=False, stop=(e == E - 1))
                    if e == E - 1:
                        mm.then_inc(s["cmb"], 1)

            pe.wait_ge(s["w1"], 16)
            pe.wait_ge(s["w2"], 16)
            pe.wait_ge(s["b2"], 16)
            pe.wait_ge(s["sre"], B)
            up(0)
            for e in range(E):
                if e + 1 < E:
                    up(e + 1)
                down(e)
                if e:
                    combine(e - 1)
            combine(E - 1)
            for h in range(2):
                pe.wait_ge(s[("ctea", "cted")[h]], 1)
                for q in range(QT):
                    t = QT * h + q
                    mm = pe.transpose(SC[h][:, q * 128:(q + 1) * 128], CT[:, t * 128:(t + 1) * 128], ident)
                mm.then_inc(s["ftr"], 1)


def kernel(**a):
    import concourse.bacc as bacc
    from concourse.bass_utils import run_bass_kernel_spmd

    a = {k: np.asarray(v) for k, v in a.items()}
    f = np.float32
    p = "L0_cond_"
    parts = [a[p + "W_up"].transpose(0, 2, 1), a[p + "W_gate"].transpose(0, 2, 1),
             a[p + "W_down"].transpose(0, 2, 1).reshape(E, 2, 128, C).transpose(0, 2, 1, 3).reshape(E, 128, 2 * C),
             a[p + "b_up"].reshape(E, 2, 128).transpose(0, 2, 1),
             a[p + "b_gate"].reshape(E, 2, 128).transpose(0, 2, 1),
             a[p + "b_down"].reshape(E, C, 1)]
    q = "L0_attn_"
    cols = [a[q + "bq"].reshape(C, 1), a[q + "bk"].reshape(C, 1), a[q + "bo"].reshape(C, 1),
            a["L0_cond2_b_base"].reshape(C, 1),
            np.repeat(a[q + "conv_w"].transpose(1, 0, 2), DH, axis=0).reshape(C, H * TAPS),
            np.repeat(a[q + "conv_b"].reshape(1, H), 128, axis=0),
            a["L0_ffn_b1"].reshape(E * NJ, 128).T, a["L0_ffn_wg"],
            np.repeat(a["cond_8"], 16, axis=1).T, np.repeat(a[q + "bv"].reshape(1, C), 128, axis=0)]
    lane = np.arange(128)
    consts = np.concatenate([
        np.eye(128), lane[:, None] <= lane[None, :],
        np.repeat((np.arange(E) + E)[None], 128, axis=0),
        lane[:, None] + CAP * np.arange(E)[None],
        np.repeat(np.arange(E * CAP)[None], 128, axis=0)], axis=1).astype(f)
    arrays = {
        "cond": a["cond_8"].reshape(1, B * E),
        "wexp": np.concatenate(parts, axis=2),
        "xT": a["x"].reshape(T, C).T,
        "wqkvo": np.stack([a[q + n].T for n in ("Wq", "Wk", "Wv", "Wo")], axis=1),
        "lora": np.stack([a["L0_cond2_As"].reshape(128, C),
                          a["L0_cond2_Bs"].transpose(0, 2, 1).reshape(128, C), a["L0_cond2_W_base"].T], axis=1),
        "cols": np.concatenate(cols, axis=1),
        "b2row": a["L0_ffn_b2"].reshape(1, E * C),
        "w1": a["L0_ffn_w1"].transpose(1, 0, 2),
        "w2": a["L0_ffn_w2"].reshape(E, NJ, 128, C).transpose(2, 0, 1, 3),
        "consts": consts,
    }
    arrays = {"in_" + k: np.ascontiguousarray(v) for k, v in arrays.items()}
    nc = bacc.Bacc("TRN2", target_bir_lowering=False, num_devices=1)
    args = [nc.dram_tensor(k, v.shape, mybir.dt.from_np(v.dtype), kind="ExternalInput").ap()
            for k, v in arrays.items()]
    out = nc.dram_tensor("out", (T, C), mybir.dt.float32, kind="ExternalOutput").ap()
    build(nc, *args, out)
    r = run_bass_kernel_spmd(nc, [arrays], core_ids=[0])
    return r.results[0]["out"].reshape(B, S, C)
```

```python
import numpy as np
import concourse.bass as bass
from concourse import mybir
from contextlib import ExitStack

B, S, C = 2, 512, 128
H, DH, TAPS = 16, 8, 3
E, HE, HID = 8, 256, 512
T = B * S
NT = T // 128
QT = S // 128
G = 4
NG = H // G
U = G * QT
RING = 8
AHEAD = 4
TURN = 6
AT_PE = {(0, 1): 12, (0, 6): 0, (0, 8): 2, (0, 10): 3, (0, 13): 6, (0, 15): 1, (1, 2): 7, (NG - 1, 6): 4,
         (NG - 1, 9): 5}
AT_ACT = {(0, 7): 0, (0, 9): 2, (0, 11): 3, (1, 3): 7, (NG - 1, 7): 4, (NG - 1, 10): 5}
AT_DVE = {(0, 2): 12, (0, 11): 3, (0, 14): 6, (1, 0): 1, (1, 1): 7, (1, 5): 8, (NG - 1, 6): 9, (NG - 1, 8): 10,
          (NG - 1, 10): 5}
CAP = T // E
VW = 32
NJ = HID // 128

BQ, BK, BO, BB, CW = 0, 1, 2, 3, 4
CB = CW + H * TAPS
B1 = CB + H
WG = B1 + E * NJ
LW = WG + E
BV = LW + B
NCOLS = BV + C
WU, EB = 0, HE
WGT = EB + 5
WD = WGT + HE
EW = WD + 2 * C
ID, TRI, IO8, IP, IOTA = 0, 128, 256, 264, 272
NCONST = IOTA + E * CAP


def build(nc, cond, wexp, xT, wqkvo, lora, cols, b2row, w1, w2, consts, out):
    f32, f32r = mybir.dt.float32, mybir.dt.float32r
    u32 = mybir.dt.uint32
    ALU, ACT, AX = mybir.AluOpType, mybir.ActivationFunctionType, mybir.AxisListType

    with ExitStack() as ctx:
        def sb(name, shape, dt=f32):
            return ctx.enter_context(nc.sbuf_tensor(name, shape, dt))

        def sem(name):
            return ctx.enter_context(nc.semaphore(name))

        banks = [ctx.enter_context(nc.psum_tensor(n, [128, 512], f32))
                 for n in ("sc0", "sc1", "sc2", "sc3", "tp0", "tp1", "pvbank", "misc")]
        SC, TP, PV, MISC = banks[0:4], banks[4:6], banks[6], banks[7]
        FRONT = [banks[0:4], banks[4:8]]

        condS = sb("condS", [1, B * E])
        cmax = sb("cmax", [1, B * 8])
        cidx = sb("cidx", [1, B * 8], u32)
        we = sb("we", [128, B, EW])
        hb = sb("hb", [128, B, 2])
        xTs = sb("xTs", [128, T])
        wq = sb("wq", [128, 5, 128])
        lo_w = sb("lo_w", [128, 3, 128])
        bs = sb("bs", [128, B, 128])
        weff = sb("weff", [128, B, 128])
        wz = sb("wz", [128, B, 128])
        bz = sb("bz", [128, B])
        col = sb("col", [128, NCOLS])
        b2s = sb("b2s", [128, E * C])
        w1s = sb("w1s", [128, E, HID])
        w2s = sb("w2s", [128, E, NJ, C])
        cst = sb("cst", [128, NCONST])
        ones = sb("ones", [128, 128])
        ones_r = sb("ones_r", [128, 128], f32r)
        tri_r = sb("tri_r", [128, 128], f32r)
        ident = cst[:, ID:ID + 128]

        RAW = sb("RAW", [128, S])
        yT = sb("yT", [128, B, S])
        Qh = sb("Qh", [128, B, S], f32r)
        Ql = sb("Ql", [128, B, S], f32r)
        Kp = sb("Kp", [128, B, S + 2])
        V = sb("V", [128, B, QT, H, DH])
        Vst = sb("Vst", [128, QT, G, VW])
        cwS = sb("cwS", [128, 2, TAPS])
        ta = sb("ta", [128, S])
        tc_ = sb("tc_", [128, S])
        td = sb("td", [128, 2, S])
        kc = sb("kc", [128, S])
        Pb = sb("Pb", [128, RING, S])
        kw, kv = Pb[:, RING - 1, :], Pb[:, RING - 2, :]
        Kh = sb("Kh", [128, 2, S], f32r)
        Kl = sb("Kl", [128, 2, S], f32r)
        spare = sb("spare", [128, 4])
        nbias = sb("nbias", [128, RING])
        PT = sb("PT", [128, G, QT, S])
        rec = sb("rec", [128, QT, 2, G // 2])
        O = sb("O", [128, QT, C])
        OT = sb("OT", [128, S])
        q32 = [RAW, OT]
        x1T, zT = yT[:, 0, :], yT[:, 1, :]
        X1 = sb("X1", [128, NT, C])
        Zh = sb("Zh", [128, NT, C], f32r)
        Zl = sb("Zl", [128, NT, C], f32r)
        lg = sb("lg", [128, QT, E])
        es = sb("es", [128, QT, E])
        eq = sb("eq", [128, QT, E])
        mask = sb("mask", [128, NT, E], f32r)
        r1 = sb("r1", [128, 7, QT])
        slot = sb("slot", [128, NT])
        gval = sb("gval", [128, NT])
        diag = sb("diag", [128, QT, 128], f32r)
        SR = sb("SR", [128, T])
        D = sb("D", [128, NT, T], f32r)
        EOh, EOl = Zh, Zl

        flat = PT[:, :, :, :].rearrange("p g k s -> p (g k s)")
        Ub = [[flat[:, (4 * b + i) * 512:(4 * b + i + 1) * 512] for i in range(2)] for b in range(B)]
        Tb = [[flat[:, (4 * b + 2 + i) * 512:(4 * b + 3 + i) * 512] for i in range(2)] for b in range(B)]
        Sb_ = [[flat[:, 4096 + (4 * b + i) * 512:4096 + (4 * b + i + 1) * 512] for i in range(2)] for b in range(B)]
        Hb = [[flat[:, 4096 + (4 * b + 2 + i) * 512:4096 + (4 * b + 3 + i) * 512] for i in range(2)] for b in range(B)]
        DT = flat[:, 0:1024]
        HT = [flat[:, 1024 + 512 * i:1536 + 512 * i].rearrange("p (j s) -> p j s", j=NJ) for i in range(2)]
        CT = flat[:, 2048:3072]
        OUT = flat[:, 3072:4096].rearrange("p (t m) -> p t m", t=NT)
        COMB = [[t[:, i, :] for t in (Qh, Ql, Kh, Kl) for i in range(2)],
                [D[:, e, 0:S] for e in range(E)]]
        EO = [ta, tc_]
        STAGE_BANK = [[MISC] * 8, [TP[0], SC[2], SC[3], TP[1], MISC, PV, SC[2], TP[0]]]

        names = """spare cond cmax cidx up0 up1 down0 down1 xt0 xt1 wq lora cols b2 w1 w2 cst outd
            hb bsc ones kpad vpad wefmm wefe
            mlp ut sm hm ymm yev qmm kmm vmm qev qhi qlo kev vev
            cw ac d kc hi lo sc mx ex tp evd eva vst pv raw
            otr rcp on o2t ote wo x1 xtr xte zmm zte ztr zhi zlo lgm nl nla nr msk cum rt
            slt gm wzm wze dg srm sre disp0 dsp dtea dted onr k0 kl0 eo hmm heva hevd eom eoh eol dt2
            cmb cte ftr fo""".split()
        s = {n: sem("s_" + n) for n in names}

        block = ctx.enter_context(nc.Block())

        @block.sync
        def _(sp):
            sp.dma_start(condS[:, :], cond).then_inc(s["cond"], 16)
            sp.dma_start(xTs[:, 0:S], xT[:, 0:S]).then_inc(s["xt0"], 16)
            sp.wait_ge(s["cidx"], B)
            for b in range(B):
                e = sp.value_load(cidx[0:1, 8 * b:8 * b + 1], min_val=0, max_val=E - 1)
                for part, at, end in (("up", 0, WGT), ("down", WGT, EW)):
                    sp.dma_start(we[:, b:b + 1, at:end], wexp[bass.ds(e, 1), :, at:end]
                                 .rearrange("e p n -> p e n")).then_inc(s[f"{part}{b}"], 16)
                if b == 0:
                    sp.dma_start(xTs[:, S:T], xT[:, S:T]).then_inc(s["xt1"], 16)
            sp.dma_start(cst[:, :], consts).then_inc(s["cst"], 16)
            sp.dma_start(w1s[:, :, :], w1).then_inc(s["w1"], 16)
            sp.dma_start(w2s[:, :, :, :], w2).then_inc(s["w2"], 16)
            sp.dma_start(b2s[:, :], b2row).then_inc(s["b2"], 16)
            rows = out.rearrange("(t p) c -> p t c", p=128)
            for t, end in ((0, 3), (3, 6), (6, NT)):
                sp.wait_ge(s["fo"], end)
                sp.dma_start(rows[:, t:end, :], OUT[:, t:end, :]).then_inc(s["outd"], 16)
            sp.wait_ge(s["outd"], 16 * 3)

        @block.gpsimd
        def _(pool):
            pool.memset(ones[:, :], 1.0).then_inc(s["ones"], 1)
            for b in range(B):
                pool.memset(Kp[:, b, 0:1], 0.0).then_inc(s["kpad"], 1)
                pool.memset(Kp[:, b, S + 1:S + 2], 0.0).then_inc(s["kpad"], 1)
            pool.memset(Vst[:, :, :, DH:DH + 1], 1.0).then_inc(s["vpad"], 1)
            pool.memset(Vst[:, :, :, DH + 1:VW], 0.0).then_inc(s["vpad"], 1)
            pool.wait_ge(s["cols"], 16)

            def fetch_taps(hd, o, n):
                src = col[:, CW + TAPS * o:CW + TAPS * (o + 1)] if isinstance(o, int) else \
                    col[:, bass.ds(CW + TAPS * o, TAPS)]
                if not isinstance(hd, int) or hd > 1:
                    pool.wait_ge(s["d"], hd - 1)
                pool.tensor_copy(cwS[:, n, :], src).then_inc(s["cw"], 1)

            def low_half(hd, n):
                pool.wait_ge(s["cw"], hd + 2)
                pool.wait_ge(s["hi"], hd + 1)
                pool.tensor_tensor(Kl[:, n, :], kc[:, :], Kh[:, n, :].bitcast(f32), ALU.subtract)\
                    .then_inc(s["lo"], 1)

            def outer_taps(hd, b, n):
                pool.tensor_scalar(ta[:, :], Kp[:, b, 0:S], cwS[:, n, 0:1], 1.0, ALU.mult, ALU.mult)\
                    .then_inc(s["ac"], 1)
                pool.tensor_scalar(tc_[:, :], Kp[:, b, 2:S + 2], cwS[:, n, 2:3], 1.0, ALU.mult, ALU.mult)\
                    .then_inc(s["ac"], 1)
                pool.wait_ge(s["ac"], 2 * hd)
                if not isinstance(hd, int) or hd >= 2:
                    pool.wait_ge(s["kc"], hd - 1)
                pool.tensor_tensor(td[:, n, :], ta[:, :], tc_[:, :], ALU.add).then_inc(s["d"], 1)

            pool.wait_ge(s["kpad"], 2 * B)
            fetch_taps(1, 1, 1)
            pool.wait_ge(s["cw"], 1)
            pool.wait_ge(s["kev"], 1)
            outer_taps(1, 0, 1)
            fetch_taps(2, 2, 0)
            pool.wait_ge(s["cw"], 2)
            outer_taps(2, 0, 0)
            fetch_taps(3, 3, 1)
            low_half(1, 1)
            outer_taps(3, 0, 1)
            pool.wait_ge(s["kev"], 2)

            def group(b, g):
                for j in range(G):
                    hd = H * b + G * g + j
                    o = G * g + j + 4
                    over = isinstance(g, int) and o >= H
                    if isinstance(g, int) and hd + 4 >= B * H:
                        if hd + 2 < B * H:
                            pool.wait_ge(s["hi"], hd + 3)
                            pool.tensor_tensor(Kl[:, j % 2, :], kc[:, :], Kh[:, j % 2, :].bitcast(f32),
                                               ALU.subtract).then_inc(s["lo"], 1)
                        continue
                    fetch_taps(hd + 4, o - H if over else o, j % 2)
                    low_half(hd + 2, j % 2)
                    outer_taps(hd + 4, b + 1 if over else b, j % 2)

            for b in range(B):
                with pool.Fori(0, NG - 1) as g:
                    group(b, g)
                group(b, NG - 1)

        @block.scalar
        def _(act):
            act.dma_start(col[:, :], cols).then_inc(s["cols"], 16)
            act.dma_start(lo_w[:, :, :], lora).then_inc(s["lora"], 16)
            act.dma_start(wq[:, :, :], wqkvo).then_inc(s["wq"], 16)

            act.wait_ge(s["spare"], 1)
            act.activation(spare[:, 2:3], spare[:, 0:1], ACT.Copy).then_inc(s["ex"], 1)
            act.activation(spare[:, 3:4], spare[:, 1:2], ACT.Copy).then_inc(s["eva"], 1)

            for b in range(B):
                act.wait_ge(s["hb"], b + 1)
                for i in range(2):
                    act.wait_ge(s["mlp"], 4 * b + i + 1)
                    act.activation(Ub[b][i], FRONT[b][i][:, :], ACT.Identity, bias=hb[:, b, i:i + 1], scale=0.5)\
                        .then_inc(s["ut"], 1)
                    act.activation(Tb[b][i], FRONT[b][i][:, :], ACT.Tanh, bias=hb[:, b, i:i + 1], scale=0.5)\
                        .then_inc(s["ut"], 1)

            def y(b):
                act.wait_ge(s["ymm"], b + 1)
                act.activation(yT[:, b, :], FRONT[b][0][:, :], ACT.Identity, bias=we[:, b, EB + 4:EB + 5])\
                    .then_inc(s["yev"], 1)

            def keys(b):
                act.wait_ge(s["kmm"], b + 1)
                act.activation(Kp[:, b, 1:S + 1], FRONT[b][1][:, :], ACT.Identity, bias=col[:, BK:BK + 1])\
                    .then_inc(s["kev"], 1)

            def high_queries(b):
                act.wait_ge(s["qev"], b + 1)
                act.activation(Qh[:, b, :], q32[b][:, :], ACT.Copy).then_inc(s["qhi"], 1)

            def high_first(hd):
                act.wait_ge(s["kc"], hd + 1)
                act.activation(Kh[:, hd, :], kc[:, :], ACT.Copy).then_inc(s["hi"], 1)

            y(0)
            y(1)
            keys(0)
            high_queries(0)
            high_first(0)
            keys(1)
            high_first(1)

            def high_half(hd, n):
                act.wait_ge(s["kc"], hd + 1)
                act.wait_ge(s["sc"], QT * (hd - 1))
                act.activation(Kh[:, n, :], kc[:, :], ACT.Copy).then_inc(s["hi"], 1)

            def exp(n, k):
                act.wait_ge(s["mx"], n + 2)
                act.activation(Pb[:, k, :], Pb[:, k, :], ACT.Exp, bias=nbias[:, k:k + 1], scale=-1.0)\
                    .then_inc(s["ex"], 1)

            def stage_values(b, g):
                act.wait_ge(s["pv"], 2 * (NG * b + g) + 1)
                src = V[:, b, :, bass.ds(G * g, G), :] if not isinstance(g, int) else \
                    V[:, b, :, G * g:G * g + G, :]
                act.activation(Vst[:, :, :, 0:DH], src, ACT.Copy).then_inc(s["vst"], 1)

            def after(b, k):
                tiles = slice(QT * b, QT * (b + 1))
                bank = STAGE_BANK[b][k]
                by_token = bank[:, :].rearrange("p (t m) -> p t m", t=QT)
                if k == 0:
                    act.wait_ge(s["o2t"], b + 1)
                    act.activation(OT[:, :], bank[:, :], ACT.Copy).then_inc(s["ote"], 1)
                elif k == 2:
                    act.wait_ge(s["zmm"], b + 1)
                    act.activation(zT, bank[:, :], ACT.Identity, bias=bz[:, b:b + 1]).then_inc(s["zte"], 1)
                elif k == 3:
                    act.wait_ge(s["nl"], b + 1)
                    act.activation(es[:, :, :], lg[:, :, :], ACT.Exp).then_inc(s["nla"], 1)
                elif k == 4:
                    act.wait_ge(s["xtr"], b + 1)
                    act.activation(X1[:, tiles, :], by_token, ACT.Copy).then_inc(s["xte"], 1)
                elif k == 5:
                    act.wait_ge(s["ztr"], b + 1)
                    act.activation(Zh[:, tiles, :], by_token, ACT.Copy).then_inc(s["zhi"], 1)
                elif k == 7:
                    act.wait_ge(s["srm"], b + 1)
                    act.activation(SR[:, S * b:S * (b + 1)], bank[:, :], ACT.Copy).then_inc(s["sre"], 1)

            def unit(b, g, u):
                n = U * (NG * b + g) + u
                hd = H * b + G * g + u // QT
                if b == 1 and isinstance(g, int) and (g, u) in AT_ACT:
                    after(0, AT_ACT[g, u])
                if u % 2 == 1:
                    act.wait_ge(s["tp"], n + 2)
                    act.activation(PT[:, u // QT % G, :, (u % QT) * 128:(u % QT + 1) * 128],
                                   TP[1][:, :].rearrange("p (k q) -> p k q", k=QT), ACT.Copy)\
                        .then_inc(s["eva"], 1)
                if not isinstance(g, int) or n + AHEAD < U * NG * B:
                    exp(n + AHEAD, (u + AHEAD) % RING)
                if u % QT == 0 and (not isinstance(g, int) or hd + 2 < B * H):
                    high_half(hd + 2, (u // QT) % 2)
                if u == 5:
                    stage_values(b, g)

            for k in range(AHEAD):
                exp(k, k)
            for u in range(TURN):
                if u == 2:
                    high_queries(1)
                elif u == 5:
                    act.wait_ge(s["vev"], B)
                    act.wait_ge(s["vpad"], 2)
                unit(0, 0, u)
            act.wait_ge(s["ones"], 1)
            act.wait_ge(s["cst"], 16)
            act.activation(ones_r[:, :], ones[:, :], ACT.Copy).then_inc(s["onr"], 1)
            act.activation(tri_r[:, :], cst[:, TRI:TRI + 128], ACT.Copy).then_inc(s["onr"], 1)
            with act.Fori(0, NG - 1) as g:
                for u in range(TURN, U + TURN):
                    unit(0, g + u // U, u % U)
            for u in range(TURN, U):
                unit(0, NG - 1, u)
            for u in range(U + TURN):
                unit(1, u // U, u % U)
            with act.Fori(1, NG - 1) as g:
                for u in range(TURN, U + TURN):
                    unit(1, g + u // U, u % U)
            for u in range(TURN, U):
                unit(1, NG - 1, u)
            for k in (0, 2, 3, 4, 5):
                after(1, k)

            act.wait_ge(s["dsp"], 1)
            act.activation(DT[:, 0:512], SC[0][:, :], ACT.Copy).then_inc(s["dtea"], 1)

            def hidden(e):
                act.wait_ge(s["hmm"], e + 1)
                if e >= 2:
                    act.wait_ge(s["eom"], e - 1)
                for j in range(NJ):
                    act.activation(HT[0][:, j, :], SC[2][:, j * 128:(j + 1) * 128], ACT.Relu,
                                   bias=col[:, B1 + NJ * e + j:B1 + NJ * e + j + 1]).then_inc(s["heva"], 1)

            after(1, 7)
            hidden(0)
            for e in range(E):
                if e % 2 == 1 and e + 1 < E:
                    hidden(e + 1)
                act.wait_ge(s["eo"], e + 1)
                act.activation(EOh[:, e, :], EO[e % 2][:, 0:C], ACT.Copy).then_inc(s["eoh"], 1)
            for i in range(NT // 2):
                act.wait_ge(s["cmb"], 1 + i // 2)
                act.activation(CT[:, i * 256:(i + 1) * 256], (PV, MISC)[i // 2][:, i % 2 * 256:(i % 2 + 1) * 256],
                               ACT.Copy).then_inc(s["cte"], 1)

        @block.vector
        def _(dve):
            dve.memset(nbias[:, 0:1], 0.0).then_inc(s["evd"], 1)
            dve.memset(nbias[:, 1:2], 0.0).then_inc(s["raw"], 1)
            dve.memset(nbias[:, 2:3], 0.0).then_inc(s["mx"], 1)
            dve.memset(nbias[:, 3:4], 0.0).then_inc(s["on"], 1)
            dve.memset(spare[:, 0:2], 0.0).then_inc(s["spare"], 1)
            dve.wait_ge(s["cond"], 16)
            for b in range(B):
                dve.max(cmax[:, 8 * b:8 * b + 8], condS[:, E * b:E * b + E]).then_inc(s["cmax"], 1)
            for b in range(B):
                dve.wait_ge(s["cmax"], b + 1)
                dve.max_index(cidx[:, 8 * b:8 * b + 8], cmax[:, 8 * b:8 * b + 8],
                              condS[:, E * b:E * b + E]).then_inc(s["cidx"], 1)
            dve.wait_ge(s["lora"], 16)
            dve.wait_ge(s["cols"], 16)
            for b in range(B):
                dve.tensor_scalar(bs[:, b, :], lo_w[:, 1, :], col[:, LW + b:LW + b + 1], 2.0,
                                  ALU.mult, ALU.mult).then_inc(s["bsc"], 1)
            for b in range(B):
                dve.wait_ge(s[f"up{b}"], 16)
                dve.tensor_scalar(hb[:, b, :], we[:, b, EB:EB + 2], 0.5, None, ALU.mult).then_inc(s["hb"], 1)
                dve.wait_ge(s["wefmm"], B)
                dve.tensor_tensor(weff[:, b, :], MISC[:, b * C:(b + 1) * C], lo_w[:, 2, :], ALU.add)\
                    .then_inc(s["wefe"], 1)

            def middle_tap(hd, b, o, n):
                at = CW + TAPS * o + 1
                w = col[:, at:at + 1] if isinstance(o, int) else col[:, bass.ds(at, 1)]
                dve.wait_ge(s["d"], hd)
                if isinstance(hd, int) and hd == 1:
                    dve.wait_ge(s["kl0"], 1)
                else:
                    dve.wait_ge(s["lo"], hd - 1)
                dve.scalar_tensor_tensor(kc[:, :], Kp[:, b, 1:S + 1], w, td[:, n, :], ALU.mult, ALU.add)\
                    .then_inc(s["kc"], 1)

            for b in range(B):
                for i in range(2):
                    dve.wait_ge(s["ut"], 4 * b + 2 * i + 2)
                    dve.scalar_tensor_tensor(Sb_[b][i], Tb[b][i], 1.0, Ub[b][i], ALU.add, ALU.mult)\
                        .then_inc(s["sm"], 1)
                for i in range(2):
                    dve.wait_ge(s["sm"], 2 * b + i + 1)
                    dve.wait_ge(s["mlp"], 4 * b + 3 + i)
                    dve.scalar_tensor_tensor(Hb[b][i], FRONT[b][2 + i][:, :], we[:, b, EB + 2 + i:EB + 3 + i],
                                             Sb_[b][i], ALU.add, ALU.mult).then_inc(s["hm"], 1)

            def queries(b):
                dve.wait_ge(s["qmm"], b + 1)
                dve.tensor_scalar(q32[b][:, :], FRONT[b][2][:, :], col[:, BQ:BQ + 1], -float(DH) ** -0.5,
                                  ALU.add, ALU.mult).then_inc(s["qev"], 1)

            def low_queries(b):
                dve.wait_ge(s["qhi"], b + 1)
                dve.tensor_tensor(Ql[:, b, :], q32[b][:, :], Qh[:, b, :].bitcast(f32), ALU.subtract)\
                    .then_inc(s["qlo"], 1)

            def values(b):
                dve.wait_ge(s["vmm"], b + 1)
                bv = col[:, BV:BV + C].rearrange("p (a c) -> p a c", a=1).broadcast_to([128, QT, C])
                dve.tensor_tensor(V[:, b, :, :, :].rearrange("p k h d -> p k (h d)"),
                                  FRONT[b][3][:, :].rearrange("p (k c) -> p k c", k=QT), bv, ALU.add)\
                    .then_inc(s["vev"], 1)

            def first_head():
                dve.wait_ge(s["kev"], 1)
                dve.wait_ge(s["kpad"], 2 * B)
                dve.tensor_scalar(kw[:, :], Kp[:, 0, 0:S], col[:, CW:CW + 1], None, ALU.mult).then_inc(s["k0"], 1)
                queries(0)
                dve.wait_ge(s["k0"], 1)
                dve.scalar_tensor_tensor(kv[:, :], Kp[:, 0, 2:S + 2], col[:, CW + 2:CW + 3], kw[:, :],
                                         ALU.mult, ALU.add).then_inc(s["k0"], 1)
                dve.wait_ge(s["k0"], 2)
                dve.scalar_tensor_tensor(kc[:, :], Kp[:, 0, 1:S + 1], col[:, CW + 1:CW + 2], kv[:, :],
                                         ALU.mult, ALU.add).then_inc(s["kc"], 1)

            first_head()
            low_queries(0)
            dve.wait_ge(s["hi"], 1)
            dve.tensor_tensor(Kl[:, 0, :], kc[:, :], Kh[:, 0, :].bitcast(f32), ALU.subtract).then_inc(s["kl0"], 1)
            middle_tap(1, 0, 1, 1)
            values(0)

            def maximum(n, k, o):
                cb = col[:, CB + o:CB + o + 1] if isinstance(o, int) else col[:, bass.ds(CB + o, 1)]
                dve.wait_ge(s["sc"], n + 1)
                dve.tensor_scalar(Pb[:, k, :], SC[k % 4][:, :], cb, None, ALU.subtract, ALU.min,
                                  accum_out=nbias[:, k:k + 1]).then_inc(s["mx"], 1)

            def raw_out(b, g):
                dve.wait_ge(s["pv"], 2 * (NG * b + g) + 1)
                dve.wait_ge(s["otr"], NG * b + g)
                dve.tensor_copy(RAW[:, :], PV[:, :]).then_inc(s["raw"], 1)

            def normalise(b, g):
                dve.wait_ge(s["otr"], NG * b + g + 1)
                t = MISC[:, :].rearrange("p (i t j w) -> p t i j w", i=2, t=QT, j=2)
                dve.reciprocal(rec[:, :, :, :], t[:, :, :, :, DH]).then_inc(s["rcp"], 1)
                dve.wait_ge(s["rcp"], NG * b + g)
                if isinstance(g, int):
                    at = (g - 1) % NG * G * DH
                    dst = O[:, :, at:at + G * DH]
                else:
                    dst = O[:, :, bass.ds(G * DH * (g - 1), G * DH)]
                for i in range(2):
                    r = rec[:, :, i, :].rearrange("p t (j a) -> p t j a", a=1).broadcast_to([128, QT, 2, DH])
                    o = dst.rearrange("p t (i j d) -> p t i j d", i=2, j=2)[:, :, i, :, :]
                    dve.tensor_tensor(o, t[:, :, i, :, 0:DH], r, ALU.mult).then_inc(s["on"], 1)

            def over_experts(a):
                return a.rearrange("p (t a) -> p t a", a=1).broadcast_to([128, QT, E])

            io8 = cst[:, IO8:IO8 + E].rearrange("p (a e) -> p a e", a=1).broadcast_to([128, QT, E])
            lmax, ssum, rs, gmax, idx, pos, s1 = (r1[:, i, :] for i in range(7))

            def after(b, k):
                tiles = slice(QT * b, QT * (b + 1))
                bank = MISC if k > 7 else STAGE_BANK[b][k]
                n = [9 * b + (6 if k == 6 else 0)]

                def step(ins):
                    n[0] += 1
                    ins.then_inc(s["nr"], 1)
                    dve.wait_ge(s["nr"], n[0])

                if k == 12:
                    dve.wait_ge(s["wzm"], 1)
                    dve.tensor_copy(wz[:, :, :], bank[:, 0:B * C].rearrange("p (b m) -> p b m", b=B))\
                        .then_inc(s["wze"], 1)
                    dve.tensor_scalar(bz[:, :], bank[:, B * C:B * C + B], col[:, BB:BB + 1], None, ALU.add)\
                        .then_inc(s["wze"], 1)
                elif k == 1:
                    dve.wait_ge(s["wo"], b + 1)
                    dve.scalar_tensor_tensor(x1T, bank[:, :], col[:, BO:BO + 1], xTs[:, S * b:S * (b + 1)],
                                             ALU.add, ALU.add).then_inc(s["x1"], 1)
                elif k == 5:
                    dve.wait_ge(s["zhi"], b + 1)
                    dve.tensor_tensor(Zl[:, tiles, :], bank[:, :].rearrange("p (t m) -> p t m", t=QT),
                                      Zh[:, tiles, :].bitcast(f32), ALU.subtract).then_inc(s["zlo"], 1)
                elif k == 3:
                    L = bank[:, 0:QT * E].rearrange("p (t e) -> p t e", e=E)
                    dve.wait_ge(s["lgm"], b + 1)
                    step(dve.tensor_reduce(lmax, L, AX.X, ALU.max))
                    dve.tensor_tensor(lg[:, :, :], L, over_experts(lmax), ALU.subtract).then_inc(s["nl"], 1)
                    dve.wait_ge(s["nla"], b + 1)
                    dve.tensor_reduce(gmax, es[:, :, :], AX.X, ALU.max).then_inc(s["gm"], 1)
                    step(dve.tensor_reduce(ssum, es[:, :, :], AX.X, ALU.add))
                    step(dve.reciprocal(rs, ssum))
                    dve.tensor_tensor(es[:, :, :], es[:, :, :], over_experts(rs), ALU.mult).then_inc(s["gm"], 1)
                    dve.wait_ge(s["gm"], 3 * b + 1)
                    dve.tensor_tensor(gmax, gmax, rs, ALU.mult).then_inc(s["gm"], 1)
                    dve.wait_ge(s["gm"], 3 * b + 3)
                    step(dve.tensor_tensor(eq[:, :, :], es[:, :, :], over_experts(gmax), ALU.is_equal))
                    step(dve.scalar_tensor_tensor(eq[:, :, :], eq[:, :, :], -float(E), io8, ALU.mult, ALU.add))
                    step(dve.tensor_reduce(idx, eq[:, :, :], AX.X, ALU.min))
                    dve.scalar_tensor_tensor(mask[:, tiles, :], io8, -float(E), over_experts(idx),
                                             ALU.add, ALU.is_equal).then_inc(s["msk"], 1)
                elif k == 6:
                    dve.wait_ge(s["cum"], b + 1)
                    cum = bank[:, 64:64 + QT * E].rearrange("p (t e) -> p t e", e=E)
                    step(dve.tensor_tensor(eq[:, :, :], cum, mask[:, tiles, :].bitcast(f32), ALU.mult))
                    step(dve.tensor_reduce(pos, eq[:, :, :], AX.X, ALU.add))
                    step(dve.scalar_tensor_tensor(s1, idx, float(CAP), pos, ALU.mult, ALU.add))
                    dve.scalar_tensor_tensor(slot[:, tiles], pos, float(CAP), s1, ALU.is_le, ALU.mult)\
                        .then_inc(s["slt"], 1)
                    dve.scalar_tensor_tensor(gval[:, tiles], pos, float(CAP), gmax, ALU.is_le, ALU.mult)\
                        .then_inc(s["rt"], 1)
                elif k == 7:
                    dve.wait_ge(s["slt"], b + 1)
                    per_token = slot[:, tiles].rearrange("p (q a) -> p q a", a=1).broadcast_to([128, QT, 128])
                    dve.tensor_tensor(diag[:, :, :], ident.rearrange("p (a c) -> p a c", a=1)
                                      .broadcast_to([128, QT, 128]), per_token, ALU.mult).then_inc(s["dg"], 1)
                elif k in (8, 9, 10, 11):
                    t = QT * b + k - 8
                    dve.wait_ge(s["slt"], b + 1)
                    dve.tensor_scalar(D[:, t, :], cst[:, IOTA:IOTA + T], slot[:, t:t + 1], None, ALU.is_equal)\
                        .then_inc(s["disp0"], 1)

            def unit(b, g, u):
                n = U * (NG * b + g) + u
                m, j = u + AHEAD, u // QT
                if not (isinstance(g, int) and b + g == 0):
                    if u == 4:
                        raw_out(b, g)
                    elif u == 5:
                        normalise(b, g)
                if b == 1 and isinstance(g, int) and (g, u) in AT_DVE:
                    after(0, AT_DVE[g, u])
                if not isinstance(g, int) or n + AHEAD < U * NG * B:
                    over = isinstance(g, int) and G * g + m // QT >= H
                    maximum(n + AHEAD, m % RING, G * g + m // QT - (H if over else 0))
                if u % 2 == 0:
                    dve.wait_ge(s["tp"], n + 2)
                    dve.tensor_copy(PT[:, j % G, :, (u % QT) * 128:(u % QT + 1) * 128],
                                    TP[0][:, :].rearrange("p (k q) -> p k q", k=QT))\
                        .then_inc(s["evd"], 1)
                if u % QT == 2 and (not isinstance(g, int) or H * b + G * g + j + 3 < B * H):
                    over = isinstance(g, int) and G * g + j + 3 >= H
                    middle_tap(H * b + G * g + j + 3, b + 1 if over else b,
                               G * g + j + 3 - (H if over else 0), (j + 1) % 2)

            for k in range(AHEAD):
                maximum(k, k, 0)
            middle_tap(2, 0, 2, 0)
            for u in range(TURN):
                if u == 1:
                    queries(1)
                elif u == 3:
                    low_queries(1)
                elif u == 5:
                    values(1)
                unit(0, 0, u)
            with dve.Fori(0, NG - 1) as g:
                for u in range(TURN, U + TURN):
                    unit(0, g + u // U, u % U)
            for u in range(TURN, U):
                unit(0, NG - 1, u)
            dve.wait_ge(s["cst"], 16)
            for u in range(U + TURN):
                unit(1, u // U, u % U)
            with dve.Fori(1, NG - 1) as g:
                for u in range(TURN, U + TURN):
                    unit(1, g + u // U, u % U)
            for u in range(TURN, U):
                unit(1, NG - 1, u)
            def spread(e, b):
                dve.tensor_scalar(COMB[b][e], SR[:, S * b:S * (b + 1)], cst[:, IP + e:IP + e + 1],
                                  None, ALU.is_equal).then_inc(s["dt2"], 1)

            dve.wait_ge(s["pv"], 4 * NG + 1)
            dve.wait_ge(s["otr"], B * NG)
            dve.tensor_copy(RAW[:, 0:384], PV[:, 0:384]).then_inc(s["raw"], 1)
            dve.wait_ge(s["pv"], 4 * NG + 2)
            dve.tensor_copy(RAW[:, 384:512], SC[3][:, 0:128]).then_inc(s["raw"], 1)
            dve.wait_ge(s["sre"], 1)
            spread(0, 0)
            spread(1, 0)
            normalise(1, NG)
            after(0, 11)
            for e in range(2, 6):
                spread(e, 0)
            for k in (1, 3, 5, 6, 8, 9, 10, 11, 7):
                after(1, k)
            spread(6, 0)
            spread(7, 0)
            dve.wait_ge(s["dsp"], 2)
            dve.tensor_copy(DT[:, 512:1024], SC[1][:, :]).then_inc(s["dted"], 1)
            dve.wait_ge(s["b2"], 16)

            for e in range(E):
                if e % 2 == 0:
                    dve.wait_ge(s["hmm"], e + 2)
                    if e >= 2:
                        dve.wait_ge(s["eom"], e)
                    for j in range(NJ):
                        at = B1 + NJ * (e + 1) + j
                        dve.tensor_scalar(HT[1][:, j, :], SC[3][:, j * 128:(j + 1) * 128],
                                          col[:, at:at + 1], 0.0, ALU.add, ALU.max).then_inc(s["hevd"], 1)
                if e == 0:
                    dve.wait_ge(s["sre"], 2)
                spread(e, 1)
                dve.wait_ge(s["eom"], e + 1)
                if e >= 2:
                    dve.wait_ge(s["eoh"], e - 1)
                    dve.wait_ge(s["eol"], e - 1)
                dve.tensor_tensor(EO[e % 2][:, 0:C], TP[e % 2][:, 0:C], b2s[:, e * C:(e + 1) * C], ALU.add)\
                    .then_inc(s["eo"], 1)
                dve.wait_ge(s["eoh"], e + 1)
                dve.tensor_tensor(EOl[:, e, :], EO[e % 2][:, 0:C], EOh[:, e, :].bitcast(f32), ALU.subtract)\
                    .then_inc(s["eol"], 1)
            for t in range(NT):
                dve.wait_ge(s["ftr"], t // 2 + 1)
                dve.scalar_tensor_tensor(OUT[:, t, :], SC[t // 2][:, t % 2 * 128:(t % 2 + 1) * 128],
                                         gval[:, t:t + 1], X1[:, t, :], ALU.mult, ALU.add).then_inc(s["fo"], 1)

        @block.tensor
        def _(pe):
            def keep_busy(bank, n):
                for _ in range(n):
                    pe.matmul(bank[:, 0:128], ones[:, :], ones[:, :], start=True, stop=True)

            pe.wait_ge(s["ones"], 1)
            keep_busy(SC[0], 10)
            pe.wait_ge(s["lora"], 16)
            for b in range(B):
                pe.wait_ge(s["bsc"], b + 1)
                pe.matmul(MISC[:, b * C:(b + 1) * C], lo_w[:, 0, :], bs[:, b, :], start=True, stop=True)\
                    .then_inc(s["wefmm"], 1)
            for b in range(B):
                pe.wait_ge(s[f"xt{b}"], 16)
                pe.wait_ge(s[f"up{b}"], 16)
                for i in range(4):
                    if i == 2:
                        pe.wait_ge(s[f"down{b}"], 16)
                    if b and i == 3:
                        pe.wait_ge(s["wefe"], B)
                    at = (WU, WGT)[i // 2] + i % 2 * 128
                    pe.matmul(FRONT[b][i][:, :], we[:, b, at:at + 128], xTs[:, S * b:S * (b + 1)],
                              start=True, stop=True).then_inc(s["mlp"], 1)
            pe.wait_ge(s["wq"], 16)

            def gated(b):
                pe.wait_ge(s["ut"], 4 * b + 2)
                for i in range(2):
                    pe.wait_ge(s["hm"], 2 * b + i + 1)
                    mm = pe.matmul(FRONT[b][0][:, :], we[:, b, WD + i * C:WD + (i + 1) * C], Hb[b][i],
                                   start=(i == 0), stop=(i == 1))
                mm.then_inc(s["ymm"], 1)

            def project(b):
                bank = FRONT[b]
                pe.wait_ge(s["yev"], b + 1)
                pe.matmul(bank[1][:, :], wq[:, 1, :], yT[:, b, :], start=True, stop=True).then_inc(s["kmm"], 1)
                pe.matmul(bank[2][:, :], wq[:, 0, :], yT[:, b, :], start=True, stop=True).then_inc(s["qmm"], 1)
                for k in range(QT):
                    mm = pe.matmul(bank[3][:, k * 128:(k + 1) * 128], yT[:, b, k * 128:(k + 1) * 128], wq[:, 2, :],
                                   start=True, stop=True)
                mm.then_inc(s["vmm"], 1)

            gated(0)
            gated(1)
            project(0)
            project(1)

            def scores(n, hd, b, u):
                k, q = u % 4, u % QT
                qh, ql = Qh[:, b, q * 128:(q + 1) * 128], Ql[:, b, q * 128:(q + 1) * 128]
                h2 = (u // QT) % 2
                if q == 0:
                    pe.wait_ge(s["hi"], hd + 1)
                    pe.wait_ge(s["lo"], hd)
                pe.wait_ge(s["mx"], n - 2)
                pe.matmul(SC[k][:, :], ql, Kh[:, h2, :], start=True, stop=False)
                pe.matmul(SC[k][:, :], qh, Kl[:, h2, :], start=False, stop=False)
                pe.matmul(SC[k][:, :], qh, Kh[:, h2, :], start=False, stop=True).then_inc(s["sc"], 1)

            def outputs(hd, j, gi, tiles):
                pe.wait_ge(s["evd"], 2 * hd + 5)
                pe.wait_ge(s["eva"], 2 * hd + 5)
                if j == 0:
                    pe.wait_ge(s["vst"], gi + 1)
                    pe.wait_ge(s["raw"], gi + 1)
                for k in tiles:
                    for f in range(2):
                        for i in range(2):
                            at = 32 * (2 * f + i)
                            x = PT[:, j + i, k, :].rearrange("p (l f c) -> p l f c", l=2, f=2)[:, :, f, :]
                            mm = pe.matmul(PV[at:at + VW, 128 * j:128 * (j + 2)], Vst[:, k, j + i, :], x,
                                           start=(k == 0), stop=(k == QT - 1))
                if k == QT - 1:
                    mm.then_inc(s["pv"], 1)

            def last_outputs(l):
                bank = (PV[:, 256:384], SC[3][:, 0:128])[l]
                pe.wait_ge(s["evd"], B * H * QT // 2 + l)
                pe.wait_ge(s["eva"], B * H * QT // 2 + l)
                for k in range(QT):
                    for f in range(2):
                        for i in range(2):
                            at, q = 32 * (2 * f + i), 2 * l + f
                            mm = pe.matmul(bank[at:at + VW, :], Vst[:, k, 2 + i, :],
                                           PT[:, 2 + i, k, q * 128:(q + 1) * 128], start=(k == 0), stop=(k == QT - 1))
                mm.then_inc(s["pv"], 1)

            def turn(bank, src, name):
                for q in range(QT):
                    mm = pe.transpose(bank[:, q * 128:(q + 1) * 128], src(q), ident)
                mm.then_inc(s[name], 1)

            def by_token(b, g):
                pe.wait_ge(s["on"], 2 * (NG * b + g) - 1)
                if b and not isinstance(g, int):
                    pe.wait_ge(s["sre"], 1)
                elif b:
                    pe.wait_ge(s["sre" if g else "wze"], 1 if g else 2)
                pe.wait_ge(s["vev"], B)
                pe.wait_ge(s["raw"], NG * b + g + 1)
                turn(MISC, lambda j: RAW[:, j * 128:(j + 1) * 128], "otr")

            def project_x(b):
                if b == 0:
                    pe.wait_ge(s["ote"], b + 1)
                pe.matmul(STAGE_BANK[b][2][:, :], weff[:, b, :], xTs[:, S * b:S * (b + 1)], start=True, stop=False)

            def after(b, k):
                bank = MISC if k > 7 else STAGE_BANK[b][k]
                if k == 12:
                    pe.wait_ge(s["on"], 2 * (NG - 1) + 1)
                    for i in range(B):
                        pe.matmul(bank[:, i * C:(i + 1) * C], wq[:, 4, :], weff[:, i, :], start=True, stop=True)
                        mm = pe.matmul(bank[:, B * C + i:B * C + i + 1], weff[:, i, :], col[:, BO:BO + 1],
                                       start=True, stop=True)
                    mm.then_inc(s["wzm"], 1)
                elif k == 0:
                    pe.wait_ge(s["on"], 2 * NG * (b + 1) + 1)
                    turn(bank, lambda q: O[:, q, :], "o2t")
                elif k == 1:
                    if b == 0:
                        pe.wait_ge(s["slt"], 1)
                    pe.wait_ge(s["ote"], b + 1)
                    pe.matmul(bank[:, :], wq[:, 3, :], OT[:, :], start=True, stop=True).then_inc(s["wo"], 1)
                elif k == 2:
                    if b == 0:
                        project_x(b)
                    pe.wait_ge(s["ote"], b + 1)
                    pe.wait_ge(s["wze"], 2)
                    pe.matmul(bank[:, :], wz[:, b, :], OT[:, :], start=False, stop=True).then_inc(s["zmm"], 1)
                elif k == 3:
                    pe.wait_ge(s["zte"], b + 1)
                    for q in range(QT):
                        mm = pe.matmul(bank[:, q * E:(q + 1) * E], zT[:, q * 128:(q + 1) * 128],
                                       col[:, WG:WG + E], start=True, stop=True)
                    mm.then_inc(s["lgm"], 1)
                elif k == 4:
                    pe.wait_ge(s["x1"], b + 1)
                    if b == 0:
                        pe.wait_ge(s["on"], 2 * (2 * NG - 1) + 1)
                    turn(bank, lambda q: x1T[:, q * 128:(q + 1) * 128], "xtr")
                elif k == 5:
                    if b == 0:
                        pe.wait_ge(s["xte"], 1)
                    turn(bank, lambda q: zT[:, q * 128:(q + 1) * 128], "ztr")
                elif k == 6:
                    pe.wait_ge(s["msk"], b + 1)
                    pe.wait_ge(s["onr"], 2)
                    at = bank[:, 64:64 + QT * E].rearrange("p (t e) -> p t e", e=E)
                    mm = pe.matmul(at, tri_r[:, :], mask[:, QT * b:QT * (b + 1), :], start=True, stop=False)
                    for p in range(QT * (b + 1) - 1):
                        first = max(p + 1 - QT * b, 0)
                        mm = pe.matmul(at[:, first:, :], ones_r[:, :],
                                       mask[:, p:p + 1, :].broadcast_to([128, QT - first, E]),
                                       start=False, stop=(p == QT * (b + 1) - 2))
                    mm.then_inc(s["cum"], 1)
                elif k == 7:
                    pe.wait_ge(s["dg"], b + 1)
                    pe.wait_ge(s["x1"], b + 1)
                    pe.matmul(bank[:, :], ones_r[:, :], diag[:, :, :], start=True, stop=True).then_inc(s["srm"], 1)

            def unit(b, g, u):
                gi = NG * b + g
                n, m = U * gi + u, u + AHEAD
                if not isinstance(g, int) or n + AHEAD < U * NG * B:
                    over = isinstance(g, int) and G * g + m // QT >= H
                    scores(n + AHEAD, H * b + G * g + m // QT, b + 1 if over else b, m)
                pe.wait_ge(s["ex"], n + 2)
                pe.wait_ge(s["evd" if u % 2 == 0 else "eva"], (U // 2) * gi + u // 2 + 1)
                for k in range(QT):
                    mm = pe.transpose(TP[u % 2][:, k * 128:(k + 1) * 128],
                                      Pb[:, u % RING, k * 128:(k + 1) * 128], ident)
                mm.then_inc(s["tp"], 1)
                if u % (2 * QT) in (1, 3) and not (isinstance(g, int) and b + g == 0 and u < QT):
                    outputs(H * b + G * g + u // QT - 2, (u // QT - 2) % G, gi - (1 if u < QT else 0),
                            (0, 1) if u % QT == 1 else (2, 3))
                if u == 4 and not (isinstance(g, int) and b + g == 0):
                    by_token(b, g)
                if b == 1 and isinstance(g, int) and (g, u) in AT_PE:
                    after(0, AT_PE[g, u])

            pe.wait_ge(s["qhi"], 1)
            pe.wait_ge(s["qlo"], 1)
            pe.wait_ge(s["hi"], 1)
            pe.wait_ge(s["kl0"], 1)
            for k in range(AHEAD):
                if k == AHEAD - 1:
                    pe.wait_ge(s["vev"], 1)
                qh, ql = Qh[:, 0, k * 128:(k + 1) * 128], Ql[:, 0, k * 128:(k + 1) * 128]
                pe.matmul(SC[k][:, :], ql, Kh[:, 0, :], start=True, stop=False)
                pe.matmul(SC[k][:, :], qh, Kl[:, 0, :], start=False, stop=False)
                pe.matmul(SC[k][:, :], qh, Kh[:, 0, :], start=False, stop=True).then_inc(s["sc"], 1)
            pe.wait_ge(s["cst"], 16)
            pe.transpose(TP[0][:, 0:128], ones[:, :], ident).then_inc(s["tp"], 1)
            pe.transpose(TP[0][:, 128:256], ones[:, :], ident).then_inc(s["pv"], 1)
            pe.transpose(TP[0][:, 256:384], ones[:, :], ident).then_inc(s["otr"], 1)
            pe.wait_ge(s["kev"], B)
            for u in range(TURN):
                unit(0, 0, u)
            pe.wait_ge(s["qev"], B)
            with pe.Fori(0, NG - 1) as g:
                for u in range(TURN, U + TURN):
                    unit(0, g + u // U, u % U)
            pe.wait_ge(s["qhi"], B)
            pe.wait_ge(s["qlo"], B)
            for u in range(TURN, U):
                unit(0, NG - 1, u)
            for u in range(U + TURN):
                unit(1, u // U, u % U)
            with pe.Fori(1, NG - 1) as g:
                for u in range(TURN, U + TURN):
                    unit(1, g + u // U, u % U)
            for u in range(TURN, U):
                if u == U - 1:
                    last_outputs(0)
                unit(1, NG - 1, u)

            def dispatch(t, h):
                pe.wait_ge(s["disp0"], t + 1)
                pe.matmul(SC[h][:, :], Zl[:, t, :], D[:, t, 512 * h:512 * (h + 1)], start=(t == 0), stop=False)
                mm = pe.matmul(SC[h][:, :], Zh[:, t, :], D[:, t, 512 * h:512 * (h + 1)],
                               start=False, stop=(t == NT - 1))
                if t == NT - 1:
                    mm.then_inc(s["dsp"], 1)

            pe.wait_ge(s["mx"], U * NG * B + 1)
            dispatch(0, 0)
            dispatch(0, 1)
            last_outputs(1)
            pe.wait_ge(s["on"], 2 * B * NG - 1)
            pe.wait_ge(s["zlo"], 1)
            for i in range(QT):
                pe.wait_ge(s["raw"], B * NG + (1 if i < QT - 1 else 2))
                mm = pe.transpose(MISC[:, i * 128:(i + 1) * 128], RAW[:, i * 128:(i + 1) * 128], ident)
            mm.then_inc(s["otr"], 1)
            dispatch(1, 0)
            dispatch(1, 1)
            after(1, 0)
            project_x(1)
            for k in (2, 1, 3, 4, 5):
                after(1, k)
            dispatch(2, 0)
            dispatch(2, 1)
            keep_busy(TP[0], 4)
            after(1, 6)
            dispatch(3, 0)
            dispatch(3, 1)
            keep_busy(TP[0], 3)
            for t in range(QT, NT):
                for h in range(2):
                    dispatch(t, h)
            after(1, 7)

            def up(e):
                pe.wait_ge(s["dtea" if e < E // 2 else "dted"], 1)
                if e >= 2:
                    pe.wait_ge(s[("heva", "hevd")[e % 2]], NJ * (e // 2))
                for j in range(NJ):
                    mm = pe.matmul(SC[2 + e % 2][:, j * 128:(j + 1) * 128], w1s[:, e, j * 128:(j + 1) * 128],
                                   DT[:, e * CAP:(e + 1) * CAP], start=True, stop=True)
                mm.then_inc(s["hmm"], 1)

            def down(e):
                if e >= 2:
                    pe.wait_ge(s["eol"], e - 1)
                bank = TP[e % 2][:, 0:C]
                for j in range(NJ):
                    pe.wait_ge(s[("heva", "hevd")[e % 2]], NJ * (e // 2) + j + 1)
                    mm = pe.matmul(bank, HT[e % 2][:, j, :], w2s[:, e, j, :], start=(j == 0), stop=(j == NJ - 1))
                mm.then_inc(s["eom"], 1)

            def combine(e):
                pe.wait_ge(s["eol"], e + 1)
                pe.wait_ge(s["dt2"], E + e + 1)
                for b, bank in enumerate((PV, MISC)):
                    m = COMB[b][e]
                    pe.matmul(bank[:, :], EOl[:, e, :], m, start=(e == 0), stop=False)
                    mm = pe.matmul(bank[:, :], EOh[:, e, :], m, start=False, stop=(e == E - 1))
                    if e == E - 1:
                        mm.then_inc(s["cmb"], 1)

            pe.wait_ge(s["w1"], 16)
            pe.wait_ge(s["w2"], 16)
            up(0)
            up(1)
            pe.wait_ge(s["sre"], B)
            for e in range(E):
                down(e)
                if e + 2 < E:
                    up(e + 2)
                if e:
                    combine(e - 1)
            combine(E - 1)
            for i in range(NT // 2):
                pe.wait_ge(s["cte"], i + 1)
                for t in range(2 * i, 2 * i + 2):
                    mm = pe.transpose(SC[i][:, t % 2 * 128:(t % 2 + 1) * 128], CT[:, t * 128:(t + 1) * 128], ident)
                mm.then_inc(s["ftr"], 1)


def kernel(**a):
    import concourse.bacc as bacc
    from concourse.bass_utils import run_bass_kernel_spmd

    a = {k: np.asarray(v) for k, v in a.items()}
    f = np.float32
    p = "L0_cond_"
    parts = [a[p + "W_up"].transpose(0, 2, 1),
             a[p + "b_up"].reshape(E, 2, 128).transpose(0, 2, 1),
             a[p + "b_gate"].reshape(E, 2, 128).transpose(0, 2, 1),
             a[p + "b_down"].reshape(E, C, 1),
             a[p + "W_gate"].transpose(0, 2, 1),
             a[p + "W_down"].transpose(0, 2, 1).reshape(E, 2, 128, C).transpose(0, 2, 1, 3).reshape(E, 128, 2 * C)]
    q = "L0_attn_"
    cols = [a[q + "bq"].reshape(C, 1), a[q + "bk"].reshape(C, 1), a[q + "bo"].reshape(C, 1),
            a["L0_cond2_b_base"].reshape(C, 1),
            np.repeat(a[q + "conv_w"].transpose(1, 0, 2), DH, axis=0).reshape(C, H * TAPS),
            np.repeat(a[q + "conv_b"].reshape(1, H), 128, axis=0),
            a["L0_ffn_b1"].reshape(E * NJ, 128).T, a["L0_ffn_wg"],
            np.repeat(a["cond_8"], 16, axis=1).T, np.repeat(a[q + "bv"].reshape(1, C), 128, axis=0)]
    lane = np.arange(128)
    consts = np.concatenate([
        np.eye(128), lane[:, None] <= lane[None, :],
        np.repeat((np.arange(E) + E)[None], 128, axis=0),
        1 + lane[:, None] + CAP * np.arange(E)[None],
        np.repeat(1 + np.arange(E * CAP)[None], 128, axis=0)], axis=1).astype(f)
    arrays = {
        "cond": a["cond_8"].reshape(1, B * E),
        "wexp": np.concatenate(parts, axis=2),
        "xT": a["x"].reshape(T, C).T,
        "wqkvo": np.stack([a[q + n].T for n in ("Wq", "Wk", "Wv", "Wo")]
                          + [a[q + "Wo"]], axis=1),
        "lora": np.stack([a["L0_cond2_As"].reshape(128, C),
                          a["L0_cond2_Bs"].transpose(0, 2, 1).reshape(128, C), a["L0_cond2_W_base"].T], axis=1),
        "cols": np.concatenate(cols, axis=1),
        "b2row": np.repeat(a["L0_ffn_b2"].reshape(1, E * C), 128, axis=0),
        "w1": a["L0_ffn_w1"].transpose(1, 0, 2),
        "w2": a["L0_ffn_w2"].reshape(E, NJ, 128, C).transpose(2, 0, 1, 3),
        "consts": consts,
    }
    arrays = {"in_" + k: np.ascontiguousarray(v) for k, v in arrays.items()}
    nc = bacc.Bacc("TRN2", target_bir_lowering=False, num_devices=1)
    args = [nc.dram_tensor(k, v.shape, mybir.dt.from_np(v.dtype), kind="ExternalInput").ap()
            for k, v in arrays.items()]
    out = nc.dram_tensor("out", (T, C), mybir.dt.float32, kind="ExternalOutput").ap()
    build(nc, *args, out)
    r = run_bass_kernel_spmd(nc, [arrays], core_ids=[0])
    return r.results[0]["out"].reshape(B, S, C)
```
